# Optimizing a Trainium2 kernel written in Bass

```python
import numpy as np
import jax
import jax.numpy as jnp

def _softmax(x, axis=-1):
    return jax.nn.softmax(x, axis=axis)

def _gelu(x):
    return jax.nn.gelu(x, approximate=True)

def _silu(x):
    return jax.nn.silu(x)

def _sigmoid(x):
    return jax.nn.sigmoid(x)

def _layernorm(x, axis=-1, eps=1e-05):
    m = jnp.mean(x, axis=axis, keepdims=True)
    v = jnp.var(x, axis=axis, keepdims=True)
    return (x - m) / jnp.sqrt(v + eps)

def _scatter_add(tgt, idx, src, axis=0):
    return tgt.at[idx].add(src)

def _segment_sum(src, seg, n):
    return jax.ops.segment_sum(src, seg, n)
kernel_name = 'mk_pixart_resid_d1_seqx_r4_71a25c'

def setup_inputs(seed: int=0):
    np.random.seed(seed)
    _w = jnp.asarray

    def _rec_inputs():
        import jax
        import jax.numpy as jnp
        _rk = jax.random.key(seed)
        x = -0.0002928 + 1 * jax.random.normal(jax.random.fold_in(_rk, 1), (4, 512, 512), jnp.float32)
        _lenS = 512 - jax.random.randint(jax.random.fold_in(_rk, 7), (4,), 0, max(1, 512 // 4) + 1, jnp.int32)
        _lenS2 = 512 - jax.random.randint(jax.random.fold_in(_rk, 8), (4,), 0, max(1, 512 // 4) + 1, jnp.int32)
        _ctx_2048P = jax.random.normal(jax.random.fold_in(_rk, 11), (4, 16, 512), jnp.float32)
        _ctx_2048c = jax.random.dirichlet(jax.random.fold_in(_rk, 511), 0.3 * jnp.ones((16,), jnp.float32), (4, 512))
        _ctx_2048t = jnp.einsum('bsk,bkd->bsd', _ctx_2048c, _ctx_2048P)
        _ctx_2048t = _ctx_2048t * jax.lax.rsqrt(jnp.mean(jnp.square(_ctx_2048t)) + 1e-12) * 0.953939
        ctx_2048 = -1.39393e-06 + 0.999914 * (_ctx_2048t + 0.3 * jax.random.normal(jax.random.fold_in(_rk, 611), (4, 512, 512), jnp.float32))
        itok_B_779_1933 = jax.random.randint(jax.random.fold_in(_rk, 12), (4,), 779, 1934, jnp.int32)
        return (x, ctx_2048, itok_B_779_1933)
    x, ctx_2048, itok_B_779_1933 = _rec_inputs()

    def _L0_xcond_setup():
        import jax, jax.numpy as jnp
        import numpy as np
        NUM_HEADS = 8
        HEAD_DIM = 64
        AVG_K_LENGTH = 20
        SCALE = 1.0 / (HEAD_DIM ** 0.5 * float(np.log(AVG_K_LENGTH)))
        key = jax.random.key(seed)
        k1, k2, k3, k4 = jax.random.split(key, 4)
        B, HD, LQ, LK = (4, NUM_HEADS * HEAD_DIM, 512, 512)
        q = jax.random.normal(k1, (B, HD, LQ), dtype=jnp.float32)
        k = jax.random.normal(k2, (B, HD, LK), dtype=jnp.float32)
        v = jax.random.normal(k3, (B, HD, LK), dtype=jnp.float32)
        k_length = jax.random.randint(k4, (B,), 128, LK + 1, dtype=jnp.int32)
        return {'q': q, 'k': k, 'v': v, 'k_length': k_length}
    _L0_xcond_all = _L0_xcond_setup()
    _L0_xcond_in = {k: v for k, v in _L0_xcond_all.items() if k in ()}
    del _L0_xcond_all

    def _L0_ffn_setup():
        import jax, jax.numpy as jnp
        import numpy as np
        B, S, D = (2, 512, 512)
        E, H, TOP_K = (8, 352, 2)
        SH = 352
        ROUTED_SCALE = 2.5
        key = jax.random.key(seed)
        ks = jax.random.split(key, 8)
        std = 0.02
        return {'x': jax.random.normal(ks[0], (B, S, D), jnp.float32), 'gate_w': jax.random.normal(ks[1], (E, D), jnp.float32) * std, 'w1': jax.random.normal(ks[2], (E, D, H), jnp.float32) * std, 'w3': jax.random.normal(ks[3], (E, D, H), jnp.float32) * std, 'w2': jax.random.normal(ks[4], (E, H, D), jnp.float32) * std, 'sw1': jax.random.normal(ks[5], (D, SH), jnp.float32) * std, 'sw3': jax.random.normal(ks[6], (D, SH), jnp.float32) * std, 'sw2': jax.random.normal(ks[7], (SH, D), jnp.float32) * std}
    _L0_ffn_all = _L0_ffn_setup()
    _L0_ffn_in = {k: v for k, v in _L0_ffn_all.items() if k in ('gate_w', 'w1', 'w2', 'w3', 'sw1', 'sw2', 'sw3')}
    del _L0_ffn_all
    return {'x': x, 'ctx_2048': ctx_2048, 'itok_B_779_1933': itok_B_779_1933, 'L0_ffn_gate_w': _L0_ffn_in['gate_w'], 'L0_ffn_w1': _L0_ffn_in['w1'], 'L0_ffn_w2': _L0_ffn_in['w2'], 'L0_ffn_w3': _L0_ffn_in['w3'], 'L0_ffn_sw1': _L0_ffn_in['sw1'], 'L0_ffn_sw2': _L0_ffn_in['sw2'], 'L0_ffn_sw3': _L0_ffn_in['sw3']}

def reference(x, ctx_2048, itok_B_779_1933, L0_ffn_gate_w, L0_ffn_w1, L0_ffn_w2, L0_ffn_w3, L0_ffn_sw1, L0_ffn_sw2, L0_ffn_sw3):
    import jax
    import jax.numpy as jnp

    def _L0_xcond_ref(q, k, v, k_length):
        import jax, jax.numpy as jnp
        import numpy as np
        NUM_HEADS = 8
        HEAD_DIM = 64
        AVG_K_LENGTH = 20
        SCALE = 1.0 / (HEAD_DIM ** 0.5 * float(np.log(AVG_K_LENGTH)))
        b, hd, lq = q.shape
        lk = k.shape[-1]
        d = hd // NUM_HEADS
        qh = q.reshape(b, NUM_HEADS, d, lq)
        kh = k.reshape(b, NUM_HEADS, d, lk)
        vh = v.reshape(b, NUM_HEADS, d, lk)
        s = SCALE * jnp.log(k_length.astype(jnp.float32))[:, None, None, None]
        attn = jnp.einsum('bhdq,bhdk->bhqk', qh, kh)
        attn = jax.nn.softmax(s * attn, axis=-1)
        out = jnp.einsum('bhqk,bhdk->bhdq', attn, vh)
        return out.reshape(b, hd, lq)

    def _L0_ffn_ref(x, gate_w, w1, w2, w3, sw1, sw2, sw3):
        import jax, jax.numpy as jnp
        import numpy as np
        B, S, D = (2, 512, 512)
        E, H, TOP_K = (8, 352, 2)
        SH = 352
        ROUTED_SCALE = 2.5
        b, s, d = x.shape
        xt = x.reshape(b * s, d)
        scores = jax.nn.sigmoid(xt @ gate_w.T)
        top_scores, top_idx = jax.lax.top_k(scores, TOP_K)
        top_scores = top_scores / (jnp.sum(top_scores, axis=-1, keepdims=True) + 1e-20)
        top_scores = top_scores * ROUTED_SCALE
        combine = jnp.sum(jax.nn.one_hot(top_idx, E, dtype=xt.dtype) * top_scores[..., None], axis=1)
        h = jnp.einsum('td,edh->eth', xt, w1)
        u = jnp.einsum('td,edh->eth', xt, w3)
        y = jnp.einsum('eth,ehd->etd', jax.nn.silu(h) * u, w2)
        routed = jnp.einsum('etd,te->td', y, combine)
        shared = jax.nn.silu(xt @ sw1) * (xt @ sw3) @ sw2
        return (routed + shared).reshape(b, s, d)
    x = x + _L0_xcond_ref(_layernorm(x, axis=-1), ctx_2048, ctx_2048, itok_B_779_1933)
    x = x + _L0_ffn_ref(_layernorm(x, axis=-1), L0_ffn_gate_w, L0_ffn_w1, L0_ffn_w2, L0_ffn_w3, L0_ffn_sw1, L0_ffn_sw2, L0_ffn_sw3)
    return x

_drawn_inputs = setup_inputs


def setup_inputs(seed=0):
    import zlib

    import numpy as np

    out = dict(_drawn_inputs(seed))
    spreads = {}
    factors = {}
    for name, (base, spread) in spreads.items():
        noise = np.random.default_rng([zlib.crc32(name.encode()), seed]).standard_normal(out[name].shape)
        drawn = base * np.exp(spread * noise) if base else spread * noise
        out[name] = jnp.asarray(drawn.astype(out[name].dtype))
    for name, factor in factors.items():
        out[name] = (out[name] * factor).astype(out[name].dtype)
    return out
```

```python
from contextlib import ExitStack

import numpy as np

import concourse.bass as bass
from concourse import mybir

ALU = mybir.AluOpType
ACT = mybir.ActivationFunctionType
AX = mybir.AxisListType
F32 = mybir.dt.float32
F32R = mybir.dt.float32r
BF16 = mybir.dt.bfloat16
I32 = mybir.dt.int32
U32 = mybir.dt.uint32

P = 128
EPS = 1e-5
HEADS = 8
DH = 64
SCALE = 1.0 / (DH ** 0.5 * float(np.log(20)))


def attention_block(nc, ctx, dims, dram, keep):
    B, C, L = dims["B"], dims["C"], dims["L"]
    NH = B * HEADS
    NT = B * C // P
    KC = L // P

    def sb(name, shape, dt=F32):
        return ctx.enter_context(nc.sbuf_tensor(name, shape, dt))

    def sem(name):
        return ctx.enter_context(nc.semaphore(name))

    x1, xt = keep["x1"], keep["xt"]
    ident, ones_f = keep["ident"], keep["ones_f"]

    xd = [sb(f"xd{p}", [P, L]) for p in range(2)]
    kd = [sb(f"kd{p}", [P, L]) for p in range(2)]
    q_f = sb("q_f", [DH, L])
    q_hi = [sb(f"q_hi{p}", [P, L], F32R) for p in range(2)]
    q_lo = [sb(f"q_lo{p}", [P, L], F32R) for p in range(2)]
    k_hl = [sb(f"k_hl{p}", [P, L], F32R) for p in range(2)]
    k_h1 = [sb(f"k_h1{p}", [P, L], F32R) for p in range(2)]
    v_t = [sb(f"v_t{p}", [P, KC, P]) for p in range(2)]
    probs = [sb(f"probs{p}", [P, KC, L]) for p in range(2)]
    diag = sb("diag", [P, KC, P], F32R)
    recip = sb("recip", [P, L])
    recip_col = sb("recip_col", [P, L // 32])
    attn = [sb(f"attn{p}", [P, L]) for p in range(2)]
    x_hat = [sb(f"x_hat{p}", [P, L]) for p in range(2)]
    neg_ident = sb("neg_ident", [P, P])
    ones_r = sb("ones_r", [P, P], F32R)
    zeros_f = sb("zeros_f", [P, L])
    stats = [sb(f"stats{p}", [P, 6]) for p in range(2)]
    mv = [sb(f"mv{p}", [P, 2]) for p in range(2)]
    rstd = [sb(f"rstd{p}", [P, 2]) for p in range(2)]
    var_e = sb("var_e", [P, 1])
    minus_half = sb("minus_half", [P, 1])
    stats2 = sb("stats2", [P, 6])
    mv2 = sb("mv2", [P, 2])
    rstd2 = sb("rstd2", [P, 2])
    qmax = [sb(f"qmax{p}", [P, KC]) for p in range(2)]
    len_i = sb("len_i", [P, B], I32)
    len_f = sb("len_f", [P, B])
    len_ln = sb("len_ln", [P, B])
    s_pair = sb("s_pair", [P, NH // 2])

    ps_max = ctx.enter_context(nc.psum_tensor("ps_max", [P, 2, L], F32))
    ps_s = ctx.enter_context(nc.psum_tensor("ps_s", [P, KC, L], F32))
    ps_o = ctx.enter_context(nc.psum_tensor("ps_o", [P, L], F32))
    ps_t = ctx.enter_context(nc.psum_tensor("ps_t", [P, KC, P], F32))

    len_landed = sem("len_landed")
    x1_landed = sem("x1_landed")
    x_landed = [sem(f"x_landed{p}") for p in range(2)]
    k_landed = [sem(f"k_landed{p}") for p in range(2)]
    pad_stored = sem("pad_stored")
    ident_zero = sem("ident_zero")
    ident_made = sem("ident_made")
    consts_made = sem("consts_made")
    len_cast = sem("len_cast")
    len_logged = sem("len_logged")
    scale_made = sem("scale_made")
    stats_raw = sem("stats_raw")
    stats_made = sem("stats_made")
    rstd_step = sem("rstd_step")
    rstd_made = sem("rstd_made")
    qhi_made = sem("qhi_made")
    khi_made = sem("khi_made")
    kh1_made = sem("kh1_made")
    qf_made = sem("qf_made")
    lows_made = sem("lows_made")
    max_ready = sem("max_ready")
    max_taken = sem("max_taken")
    diag_made = sem("diag_made")
    row_ready = sem("row_ready")
    row_made = sem("row_made")
    vt_ready = sem("vt_ready")
    v_made = sem("v_made")
    s_ready = sem("s_ready")
    exp_done = sem("exp_done")
    pv_done = sem("pv_done")
    recip_made = sem("recip_made")
    attn_made = sem("attn_made")
    x1_made = sem("x1_made")
    stats2_raw = sem("stats2_raw")
    stats2_made = sem("stats2_made")
    rstd2_made = sem("rstd2_made")
    xhat_made = sem("xhat_made")
    xhat_stored = sem("xhat_stored")
    xt_ready = sem("xt_ready")
    xt_made = sem("xt_made")
    pool_passed, act_passed, dve_passed, sp_passed = (sem(f"{e}_passed") for e in ("pool", "act", "dve", "sp"))

    x_rows = dram["x"].rearrange("b (h d) l -> (b h) d l", d=DH)
    c_rows = dram["ctx"].rearrange("b (h d) l -> (b h) d l", d=DH)
    xn_rows = dram["xn"]
    head_rows = [slice(0, DH), slice(DH, P)]

    block = ctx.enter_context(nc.Block("attention"))

    @block.sync
    def _(sp):
        def load(n, i, p):
            if not isinstance(n, int) or n >= 2:
                heads, halves = i * 2 + (p - 1), i * 4 + 2 * (p - 1)
                if not isinstance(n, int):
                    heads, halves = sp.snap(heads), sp.snap(halves)
                sp.wait_ge(lows_made, halves)
                sp.wait_ge(kh1_made, heads)
                sp.wait_ge(vt_ready, heads)
                sp.sem_inc(sp_passed, 1)
            for half in head_rows:
                sp.dma_start(xd[p][half, :], x_rows[n]).then_inc(x_landed[p], 16)
            for half in head_rows:
                sp.dma_start(kd[p][half, :], c_rows[n]).then_inc(k_landed[p], 16)

        def store(t, p):
            sp.wait_ge(xhat_made, t + 1)
            sp.dma_start(xn_rows[bass.ts(t, P), :], x_hat[p][:, :]).then_inc(xhat_stored, 16)

        load(0, 0, 0)
        load(1, 0, 1)
        sp.dma_start(len_i[:, :], dram["lengths"].partition_broadcast(P)).then_inc(len_landed, 16)
        sp.dma_start(x1[:, :, :], dram["x"].rearrange("b (t p) l -> p (b t) l", p=P)).then_inc(x1_landed, 16)
        load(2, 1, 0)
        load(3, 1, 1)
        sp.wait_ge(consts_made, 1)
        sp.dma_start(xn_rows[NT * P:NT * P + P, :], zeros_f[:, :]).then_inc(pad_stored, 16)
        sp.dma_start(dram["out"][NT * P:NT * P + P, :], zeros_f[:, :]).then_inc(pad_stored, 16)
        load(4, 2, 0)
        load(5, 2, 1)
        with sp.Fori(0, (NT - 4) // 2) as k:
            for u in range(2):
                i = k * 2 + (3 + u)
                load(i * 2, i, 0)
                load(i * 2 + 1, i, 1)
                store(k * 2 + u, u)
        load(NH - 2, NT - 1, 0)
        load(NH - 1, NT - 1, 1)
        for t in range(NT - 4, NT):
            store(t, t % 2)
        sp.wait_ge(xhat_stored, 16 * NT)
        sp.wait_ge(pad_stored, 32)

    @block.gpsimd
    def _(pool):
        nc.gpsimd.memset(ident[:, :], 0.0).then_inc(ident_zero, 1)
        pool.wait_ge(ident_zero, 1)
        nc.gpsimd.affine_select(out=ident[:, :], in_=ident[:, :], compare_op=ALU.not_equal, fill=1.0, base=0,
                                pattern=[[-1, P]], channel_multiplier=1).then_inc(ident_made, 1)
        nc.gpsimd.memset(minus_half[:, :], -0.5).then_inc(ident_zero, 1)
        pool.wait_ge(ident_zero, 2)

        def inverse_sigma(made, count, mean_var, out):
            nc.gpsimd.tensor_scalar(var_e[:, :], mean_var[:, 1:2], EPS, None, ALU.add).then_inc(rstd_step, 1)
            pool.wait_ge(rstd_step, count * 2 + 1)
            nc.gpsimd.tensor_tensor(out[:, 0:1], var_e[:, :], minus_half[:, :], ALU.pow).then_inc(rstd_step, 1)
            pool.wait_ge(rstd_step, count * 2 + 2)
            pool.sem_inc(pool_passed, 1)
            nc.gpsimd.tensor_scalar(out[:, 1:2], mean_var[:, 0:1], out[:, 0:1], -1.0, ALU.mult,
                                    ALU.mult).then_inc(made, 1)

        def head_sigma(i, p, calls):
            pool.wait_ge(stats_made, 2 * i + p + 1)
            pool.sem_inc(pool_passed, 1)
            inverse_sigma(rstd_made, calls, mv[p], rstd[p])

        def add_attention(i, p):
            pool.wait_ge(attn_made, 2 * i + p + 1)
            rows = head_rows[p]
            nc.gpsimd.tensor_tensor(x1[rows, i, :], x1[rows, i, :], attn[p][rows, :], ALU.add).then_inc(x1_made, 1)
            pool.wait_ge(x1_made, 2 * i + p + 1)

        def tile_sigma(t, calls):
            pool.wait_ge(stats2_made, t + 1)
            pool.sem_inc(pool_passed, 1)
            inverse_sigma(rstd2_made, calls, mv2, rstd2)

        for n in range(4):
            head_sigma(n // 2, n % 2, n)
        pool.wait_ge(x1_landed, 16)
        add_attention(0, 0)
        head_sigma(2, 0, 4)
        with pool.Fori(1, NT - 2) as i:
            add_attention(i - 1, 1)
            head_sigma(i + 1, 1, i * 3 + 2)
            tile_sigma(i - 1, i * 3 + 3)
            add_attention(i, 0)
            head_sigma(i + 2, 0, i * 3 + 4)
        i = NT - 2
        add_attention(i - 1, 1)
        head_sigma(i + 1, 1, i * 3 + 2)
        tile_sigma(i - 1, i * 3 + 3)
        add_attention(i, 0)
        add_attention(i, 1)
        tile_sigma(i, i * 3 + 4)
        add_attention(i + 1, 0)
        add_attention(i + 1, 1)
        tile_sigma(i + 1, i * 3 + 5)

    @block.scalar
    def _(act):
        act.wait_ge(len_cast, 1)
        nc.scalar.activation(len_ln[:, :], len_f[:, :], ACT.Ln).then_inc(len_logged, 1)

        def highs(i, p):
            act.wait_ge(rstd_made, 2 * i + p + 1)
            act.wait_ge(x_landed[p], 32 * (i + 1))
            if not isinstance(i, int) or i >= 1:
                act.wait_ge(s_ready, 2 * (2 * i + p - 1))
            nc.scalar.activation(q_hi[p][:, :], xd[p][:, :], ACT.Identity, scale=rstd[p][:, 0:1],
                                 bias=rstd[p][:, 1:2]).then_inc(qhi_made, 1)
            act.wait_ge(k_landed[p], 32 * (i + 1))
            nc.scalar.activation(k_hl[p][:, :], kd[p][:, :], ACT.Copy).then_inc(khi_made, 1)
            nc.scalar.activation(k_h1[p][0:DH, :], kd[p][0:DH, :], ACT.Copy).then_inc(kh1_made, 1)

        def values(i, p):
            act.wait_ge(vt_ready, 2 * i + p + 1)
            if not isinstance(i, int) or i >= 1:
                act.wait_ge(pv_done, 2 * i + p - 1)
            nc.scalar.activation(v_t[p][:, :, head_rows[p]], ps_t[:, :, 0:DH], ACT.Copy).then_inc(v_made, 1)

        def max_row(i, p):
            act.wait_ge(row_ready, 2 * i + p + 1)
            nc.scalar.activation(q_lo[p][DH:DH + 1, :], ps_max[DH:DH + 1, 0, :], ACT.Copy).then_inc(row_made, 1)

        def exponents(i, p):
            if not isinstance(i, int) or i >= 1:
                act.wait_ge(pv_done, 2 * i + p - 1)
            for half in range(2):
                c = slice(half * KC // 2, (half + 1) * KC // 2)
                act.wait_ge(s_ready, 2 * (2 * i + p) + half + 1)
                act.sem_inc(act_passed, 1)
                nc.scalar.activation(probs[p][:, c, :], ps_s[:, c, :], ACT.Exp,
                                     scale=s_pair[:, bass.ts(i, 1)]).then_inc(exp_done, 1)

        def tile_high(t):
            act.wait_ge(xt_ready, t + 1)
            nc.scalar.activation(xt[:, :, bass.ts(t, P)], ps_t[:, :, :], ACT.Copy).then_inc(xt_made, 1)

        act.wait_ge(consts_made, 1)
        highs(0, 0)
        values(0, 0)
        max_row(0, 0)
        highs(0, 1)
        values(0, 1)
        max_row(0, 1)
        act.wait_ge(scale_made, 1)

        def step(i, p, tile=None):
            exponents(*((i, 1) if p == 0 else (i + 1, 0)))
            if tile is not None:
                tile_high(tile)
            highs(*((i + 1, 1) if p == 0 else (i + 2, 0)))
            max_row(i + 1, p)
            values(i + 1, p)

        exponents(0, 0)
        highs(1, 0)
        step(0, 0)
        step(0, 1)
        step(1, 0)
        step(1, 1)
        with act.Fori(2, NT - 2) as i:
            step(i, 0, i - 2)
            step(i, 1)
        i = NT - 2
        step(i, 0, i - 2)
        exponents(i + 1, 0)
        max_row(i + 1, 1)
        values(i + 1, 1)
        exponents(i + 1, 1)
        for t in range(NT - 3, NT):
            tile_high(t)

    @block.vector
    def _(dve):
        nc.vector.memset(zeros_f[:, :], 0.0).then_inc(consts_made, 1)
        nc.vector.memset(ones_f[:, :], 1.0)
        for p in range(2):
            last = nc.vector.memset(v_t[p][:, :, head_rows[1 - p]], 1.0)
        last.then_inc(consts_made, 1)
        dve.wait_ge(consts_made, 2)
        nc.vector.tensor_copy(ones_r[:, :], ones_f[:, :])
        for p in range(2):
            nc.vector.tensor_copy(q_lo[p][DH:96, :], zeros_f[DH:96, :])
            nc.vector.tensor_copy(k_h1[p][DH:96, :], zeros_f[DH:96, :]).then_inc(consts_made, 1)
        dve.wait_ge(consts_made, 4)
        for p in range(2):
            nc.vector.tensor_scalar(k_h1[p][DH:DH + 1, :], zeros_f[DH:DH + 1, :], 1.0, None,
                                    ALU.add).then_inc(consts_made, 1)
        dve.wait_ge(ident_made, 1)
        nc.vector.tensor_scalar(neg_ident[:, :], ident[:, :], -1.0, None, ALU.mult).then_inc(consts_made, 1)
        dve.wait_ge(len_landed, 16)
        nc.vector.tensor_copy(len_f[:, :], len_i[:, :]).then_inc(len_cast, 1)

        def head_stats(i, p):
            dve.wait_ge(x_landed[p], 32 * (i + 1))
            nc.vector.bn_stats(stats[p][:, :], xd[p][:, :]).then_inc(stats_raw, 1)
            if not isinstance(i, int) or i >= 1:
                dve.wait_ge(rstd_made, 2 * i + p - 1)
            dve.wait_ge(stats_raw, 2 * i + p + 1)
            dve.sem_inc(dve_passed, 1)
            nc.vector.bn_aggr(mv[p][:, :], stats[p][:, :]).then_inc(stats_made, 1)

        def lows(i, p):
            dve.wait_ge(rstd_made, 2 * i + p + 1)
            nc.vector.tensor_scalar(q_f[:, :], xd[p][0:DH, :], rstd[p][0:DH, 0:1], rstd[p][0:DH, 1:2], ALU.mult,
                                    ALU.add).then_inc(qf_made, 1)
            dve.wait_ge(qhi_made, 2 * i + p + 1)
            dve.wait_ge(qf_made, 2 * i + p + 1)
            nc.vector.tensor_tensor(q_lo[p][0:DH, :], q_f[:, :], q_hi[p][0:DH, :].bitcast(F32),
                                    ALU.subtract).then_inc(lows_made, 1)
            dve.wait_ge(khi_made, 2 * i + p + 1)
            nc.vector.tensor_tensor(k_hl[p][DH:P, :], kd[p][DH:P, :], k_hl[p][DH:P, :].bitcast(F32),
                                    ALU.subtract).then_inc(lows_made, 1)

        def take_max(i, p, half):
            dve.wait_ge(max_ready, 2 * (2 * i + p) + half + 1)
            nc.vector.tensor_reduce(qmax[p][:, 2 * half:2 * half + 2], ps_max[:, :, :], AX.X,
                                    ALU.max).then_inc(max_taken, 1)

        def spread_max(i, p):
            dve.wait_ge(max_taken, 2 * (2 * i + p) + 2)
            if not isinstance(i, int) or i >= 1 or p:
                dve.wait_ge(row_ready, 2 * i + p)
            nc.vector.tensor_tensor(diag[:, :, :], neg_ident[:, :].unsqueeze(1).to_broadcast([P, KC, P]),
                                    qmax[p][:, :].unsqueeze(2).to_broadcast([P, KC, P]),
                                    ALU.mult).then_inc(diag_made, 1)

        def normalize(i, p):
            rows, sums = head_rows[p], head_rows[1 - p]
            turned = recip[rows, :].rearrange("p (b c) -> p b c", c=32)
            dve.wait_ge(pv_done, 2 * i + p + 1)
            nc.vector.transpose(recip[rows, :], ps_o[sums, :]).then_inc(recip_made, 1)
            dve.wait_ge(recip_made, 3 * (2 * i + p) + 1)
            nc.vector.reciprocal(recip_col[rows, :], turned[:, :, 0]).then_inc(recip_made, 1)
            dve.wait_ge(recip_made, 3 * (2 * i + p) + 2)
            nc.vector.transpose(recip[rows, :],
                                recip_col[rows, :].unsqueeze(2).to_broadcast([DH, L // 32, 32])).then_inc(recip_made, 1)
            dve.wait_ge(recip_made, 3 * (2 * i + p) + 3)
            if not isinstance(i, int) or i >= 1:
                dve.wait_ge(x1_made, 2 * i + p - 1)
            nc.vector.tensor_tensor(attn[p][rows, :], ps_o[rows, :], recip[rows, :],
                                    ALU.mult).then_inc(attn_made, 1)

        def tile_stats(t):
            dve.wait_ge(x1_made, 2 * t + 2)
            nc.vector.bn_stats(stats2[:, :], x1[:, t, :]).then_inc(stats2_raw, 1)
            dve.wait_ge(stats2_raw, t + 1)
            dve.sem_inc(dve_passed, 1)
            nc.vector.bn_aggr(mv2[:, :], stats2[:, :]).then_inc(stats2_made, 1)

        def tile_norm(t, p):
            dve.wait_ge(rstd2_made, t + 1)
            if not isinstance(t, int) or t >= 1:
                dve.wait_ge(xhat_stored, 16 * t)
                dve.wait_ge(xt_ready, t)
            nc.vector.tensor_scalar(x_hat[p][:, :], x1[:, t, :], rstd2[:, 0:1], rstd2[:, 1:2], ALU.mult,
                                    ALU.add).then_inc(xhat_made, 1)

        for n in range(2):
            head_stats(0, n)
            lows(0, n)
            if n == 0:
                dve.wait_ge(len_logged, 1)
                nc.vector.tensor_scalar(s_pair[:, :].rearrange("p (b h) -> p b h", b=B),
                                        len_ln[:, :].unsqueeze(2).to_broadcast([P, B, HEADS // 2]), SCALE, None,
                                        ALU.mult).then_inc(scale_made, 1)
            take_max(0, n, 0)
            take_max(0, n, 1)
            spread_max(0, n)
        head_stats(1, 0)
        lows(1, 0)

        def step(i, p):
            if p or not isinstance(i, int) or i >= 1:
                normalize(*((i - 1, 1) if p == 0 else (i, 0)))
            head_stats(*((i + 1, 1) if p == 0 else (i + 2, 0)))
            take_max(i + 1, p, 0)
            take_max(i + 1, p, 1)
            spread_max(i + 1, p)
            lows(*((i + 1, 1) if p == 0 else (i + 2, 0)))

        step(0, 0)
        step(0, 1)
        step(1, 0)
        tile_stats(0)
        step(1, 1)
        tile_norm(0, 0)
        with dve.Fori(0, (NT - 4) // 2) as k:
            for u in range(2):
                i = k * 2 + (2 + u)
                step(i, 0)
                tile_stats(k * 2 + (1 + u))
                step(i, 1)
                tile_norm(k * 2 + (1 + u), 1 - u)
        i = NT - 2
        step(i, 0)
        tile_stats(i - 1)
        normalize(i, 0)
        take_max(i + 1, 1, 0)
        take_max(i + 1, 1, 1)
        spread_max(i + 1, 1)
        tile_norm(i - 1, (i - 1) % 2)
        normalize(i, 1)
        tile_stats(i)
        tile_norm(i, i % 2)
        normalize(i + 1, 0)
        normalize(i + 1, 1)
        tile_stats(i + 1)
        tile_norm(i + 1, (i + 1) % 2)

    @block.tensor
    def _(pe):
        def max_scores(i, p, half):
            pe.wait_ge(lows_made, 2 * (2 * i + p) + 2)
            if half or p or not isinstance(i, int) or i >= 1:
                pe.wait_ge(max_taken, 2 * (2 * i + p) + half)
            if half == 0 and (p or not isinstance(i, int) or i >= 1):
                pe.wait_ge(row_made, 2 * i + p)
            for j in range(2):
                last = nc.tensor.matmul(ps_max[:, j, :], q_hi[p][:, bass.ts(2 * half + j, P)], k_hl[p][:, :],
                                        start=True, stop=True)
            last.then_inc(max_ready, 1)

        def turn_values(i, p, after_tile=None):
            pe.wait_ge(k_landed[p], 32 * (i + 1))
            if p or not isinstance(i, int) or i >= 1:
                pe.wait_ge(v_made, 2 * i + p)
            if after_tile is not None:
                pe.wait_ge(xt_made, after_tile + 1)
            for c in range(KC):
                last = nc.tensor.transpose(ps_t[:, c, :], kd[p][:, bass.ts(c, P)], ident[:, :])
            last.then_inc(vt_ready, 1)

        def spread_row(i, p):
            pe.wait_ge(diag_made, 2 * i + p + 1)
            nc.tensor.matmul(ps_max[:, 0, :], ones_r[:, :], diag[:, :, :], start=True,
                             stop=True).then_inc(row_ready, 1)

        def scores(i, p):
            pe.wait_ge(row_made, 2 * i + p + 1)
            pe.wait_ge(kh1_made, 2 * i + p + 1)
            if p or not isinstance(i, int) or i >= 1:
                pe.wait_ge(exp_done, 2 * (2 * i + p))
            for c in range(KC):
                nc.tensor.matmul(ps_s[:, c, :], k_hl[p][:, bass.ts(c, P)], q_hi[p][:, :], start=True, stop=False)
                last = nc.tensor.matmul(ps_s[:, c, :], k_h1[p][0:96, bass.ts(c, P)], q_lo[p][0:96, :],
                                        start=False, stop=True)
                if c % 2:
                    last.then_inc(s_ready, 1)

        def weigh_values(i, p, chunks):
            for c in chunks:
                if c == 0:
                    pe.wait_ge(v_made, 2 * i + p + 1)
                    if p or not isinstance(i, int) or i >= 1:
                        pe.wait_ge(attn_made, 2 * i + p)
                if c % 2 == 0:
                    pe.wait_ge(exp_done, 2 * (2 * i + p) + c // 2 + 1)
                last = nc.tensor.matmul(ps_o[:, :], v_t[p][:, c, :], probs[p][:, c, :], start=c == 0,
                                        stop=c == KC - 1)
            if KC - 1 in chunks:
                last.then_inc(pv_done, 1)

        def turn_tile(t, p, copied):
            pe.wait_ge(xhat_made, t + 1)
            pe.wait_ge(v_made, copied)
            for c in range(KC):
                last = nc.tensor.transpose(ps_t[:, c, :], x_hat[p][:, bass.ts(c, P)], ident[:, :])
            last.then_inc(xt_ready, 1)

        pe.wait_ge(ident_made, 1)
        pe.wait_ge(consts_made, 7)
        for n in range(2):
            max_scores(0, n, 0)
            turn_values(0, n)
            max_scores(0, n, 1)
            spread_row(0, n)
        scores(0, 0)

        def step(i, p, tile=None, buffer=0):
            scores(*((i, 1) if p == 0 else (i + 1, 0)))
            max_scores(i + 1, p, 0)
            if tile is not None:
                turn_tile(tile, buffer, 2 * i + 2)
            weigh_values(i, p, [0])
            max_scores(i + 1, p, 1)
            turn_values(i + 1, p, tile)
            weigh_values(i, p, [1, 2])
            spread_row(i + 1, p)
            weigh_values(i, p, [3])

        step(0, 0)
        step(0, 1)
        step(1, 0)
        step(1, 1)
        with pe.Fori(0, (NT - 4) // 2) as k:
            for u in range(2):
                i = k * 2 + (2 + u)
                step(i, 0, k * 2 + u, u)
                step(i, 1)
        i = NT - 2
        step(i, 0, i - 2, i % 2)
        scores(i + 1, 0)
        max_scores(i + 1, 1, 0)
        weigh_values(i, 1, [0])
        max_scores(i + 1, 1, 1)
        turn_values(i + 1, 1)
        weigh_values(i, 1, [1, 2])
        spread_row(i + 1, 1)
        weigh_values(i, 1, [3])
        scores(i + 1, 1)
        turn_tile(i - 1, (i - 1) % 2, NH)
        weigh_values(i + 1, 0, range(KC))
        weigh_values(i + 1, 1, range(KC))
        for t in range(NT - 2, NT):
            pe.wait_ge(xt_made, t)
            turn_tile(t, t % 2, NH)



def experts_block(nc, ctx, dims, dram, keep):
    T, L, E, H = dims["T"], dims["L"], dims["E"], dims["H"]
    NT = T // P
    GROUP = 2 * P
    NS = T // GROUP
    NX = 2 * T // GROUP + E - 1
    KC = L // P
    MH = -(-H // P)
    HR = [min(P, H - m * P) for m in range(MH)]
    assert NS == 8 and NX % 2 == 1 and KC == 4 and MH == 3 and E == 8

    def sb(name, shape, dt=F32):
        return ctx.enter_context(nc.sbuf_tensor(name, shape, dt))

    def ps(name, shape, dt=F32):
        return ctx.enter_context(nc.psum_tensor(name, shape, dt))

    def sem(name):
        return ctx.enter_context(nc.semaphore(name))

    x1, xt, ident, ones_f = keep["x1"], keep["xt"], keep["ident"], keep["ones_f"]

    w1_f, w3_f, w2_f = sb("w1_f", [P, KC, H]), sb("w3_f", [P, KC, H]), sb("w2_f", [P, MH, L])
    w1_hi, w3_hi, w2_hi = ([sb(f"w{n}_hi{p}", [P, c, f], F32R) for p in range(2)]
                           for n, c, f in ((1, KC, H), (3, KC, H), (2, MH, L)))
    w1_lo, w3_lo, w2_lo = ([sb(f"w{n}_lo{p}", [P, c, f], F32R) for p in range(2)]
                           for n, c, f in ((1, KC, H), (3, KC, H), (2, MH, L)))
    x_hi = sb("x_hi", [P, KC, GROUP], F32R)
    x_lo = sb("x_lo", [P, KC, GROUP], F32R)
    x_rows = [[sb(f"x_rows{p}{j}", [P, L]) for j in range(2)] for p in range(2)]
    silu = sb("silu", [P, MH, GROUP])
    g_f = sb("g_f", [P, MH, GROUP])
    g_hi = sb("g_hi", [P, MH, GROUP], F32R)
    g_lo = sb("g_lo", [P, MH, GROUP], F32R)
    y_sb = [sb(f"y_sb{j}", [P, L]) for j in range(2)]
    slots = [sb(f"slots{p}", [P, 2, 2], U32) for p in range(2)]

    gate_sb = sb("gate_sb", [E, L])
    gate_t = sb("gate_t", [P, KC, E])
    logits_t = sb("logits_t", [E, T])
    e_neg = sb("e_neg", [P, NT, E])
    e_one = sb("e_one", [P, NT, E])
    score = sb("score", [P, NT, E])
    top = sb("top", [P, NT, 8])
    top_i = sb("top_i", [P, NT, 8], U32)
    top_f = sb("top_f", [P, NT, 2])
    iota_e = sb("iota_e", [P, E])
    chosen = [sb(f"chosen{j}", [P, NT, E]) for j in range(2)]
    either = sb("either", [P, NT, E], BF16)
    top_sum = sb("top_sum", [P, NT])
    top_inv = sb("top_inv", [P, NT])
    upper = sb("upper", [P, P], BF16)
    ones_b = sb("ones_b", [P, P], BF16)
    running = sb("running", [P, E, NT])
    before = sb("before", [P, E])
    count = sb("count", [P, E])
    need = sb("need", [P, E])
    need_up = sb("need_up", [P, E])
    ends = sb("ends", [P, E])
    starts = sb("starts", [P, E])
    place_a = sb("place_a", [P, E, NT])
    place_b = sb("place_b", [P, E, NT])
    place_c = sb("place_c", [P, E, NT])
    picked = [sb(f"picked{j}", [P, NT, E]) for j in range(2)]
    dest_f = sb("dest_f", [P, 2, NT])
    dest = sb("dest", [P, 2, NT], U32)
    entry = sb("entry", [P, NT, 2, 2], U32)
    iota_g = sb("iota_g", [1, NX + 1])
    past = sb("past", [1, NX + 1, E])
    group_f = sb("group_f", [1, NX + 1])
    group_e = sb("group_e", [1, NX + 1], I32)
    table = sb("table", [P, 2 * NX, 2], U32)

    ps_h = [ps(f"ps_h{m}", [P, 2, GROUP]) for m in range(MH)]
    ps_y = [ps(f"ps_y{j}", [P, L]) for j in range(2)]
    ps_x = [ps(f"ps_x{j}", [P, KC, P]) for j in range(2)]
    ps_r = ps("ps_r", [P, 4, P])

    names = """gate_landed gate_turned gate_made logits_ready logits_made logits_turned exp_made score_step
        top_made entry_iota iota_made either_made ranks_ready route_step dest_made group_made consts_set upper_zero
        upper_made table_preset table_filled table_landed xhi_made xlo_made hu_ready silu_made gf_made ghi_made
        glo_made y_ready y_taken out_stored whi_made wlo_made slots_made turned add_done w2_landed w1_landed
        w3_landed entry_made gather_passed""".split()
    S = {n: sem(n) for n in names}
    x_landed = [sem(f"rows_landed{p}") for p in range(2)]

    out, xn, slot_table = dram["out"], dram["xn"], dram["slots"]
    block = ctx.enter_context(nc.Block("experts"))

    def peeled(v):
        return isinstance(v, int)

    @block.sync
    def _(sp):
        def load_weights(k, w1, w3, w2):
            if not peeled(k) or k:
                sp.wait_ge(S["wlo_made"], 4 * k - 3)
            sp.dma_start(w1_f[:, :, :], w1.rearrange("(c p) h -> p c h", p=P)).then_inc(S["w1_landed"], 16)
            if not peeled(k) or k:
                sp.wait_ge(S["wlo_made"], 4 * k - 2)
            sp.dma_start(w3_f[:, :, :], w3.rearrange("(c p) h -> p c h", p=P)).then_inc(S["w3_landed"], 16)
            if not peeled(k) or k:
                sp.wait_ge(S["wlo_made"], 4 * k)
            full = (MH - 1) * P
            sp.dma_start(w2_f[:, 0:MH - 1, :],
                         w2[0:full].rearrange("(m p) n -> p m n", p=P)).then_inc(S["w2_landed"], 16)
            sp.dma_start(w2_f[0:HR[-1], MH - 1, :], w2[full:H]).then_inc(S["w2_landed"], 16)

        def load_group(s):
            e = sp.value_load(group_e[0:1, bass.ds(s, 1)], min_val=0, max_val=E - 1)
            load_weights(s + 1, dram["w1"][e], dram["w3"][e], dram["w2"][e])

        def store(t):
            sp.wait_ge(S["y_taken"], t + 1)
            sp.dma_start(out[bass.ts(t, P), :], x1[:, t, :]).then_inc(S["out_stored"], 16)

        sp.dma_start(gate_sb[:, :], dram["gate"]).then_inc(S["gate_landed"], 16)
        load_weights(0, dram["sw1"], dram["sw3"], dram["sw2"])
        with sp.Fori(0, 2 * NS - 4) as t:
            store(t)
        sp.wait_ge(S["group_made"], 1)
        load_group(0)
        for t in range(2 * NS - 4, 2 * NS):
            store(t)
        with sp.Fori(1, NX) as s:
            load_group(s)

    @block.gpsimd
    def _(pool):
        nc.gpsimd.memset(upper[:, :], 1.0).then_inc(S["upper_zero"], 1)
        pool.wait_ge(S["upper_zero"], 1)
        nc.gpsimd.affine_select(out=upper[:, :], in_=upper[:, :], compare_op=ALU.is_gt, fill=0.0, base=0,
                                pattern=[[1, P]], channel_multiplier=-1).then_inc(S["upper_made"], 1)
        nc.gpsimd.iota(iota_e[:, :], [[1, E]], base=0, channel_multiplier=0,
                       allow_small_or_imprecise_dtypes=True).then_inc(S["iota_made"], 1)
        nc.gpsimd.iota(iota_g[:, :], [[1, NX + 1]], base=0, channel_multiplier=0,
                       allow_small_or_imprecise_dtypes=True).then_inc(S["iota_made"], 1)
        nc.gpsimd.iota(entry[:, :, :, 0], [[P, NT], [0, 2]], base=0, channel_multiplier=1).then_inc(S["entry_iota"], 1)
        nc.gpsimd.iota(table[:, :, 0], [[0, 2 * NX]], base=T, channel_multiplier=1).then_inc(S["entry_iota"], 1)
        nc.gpsimd.iota(table[:, :, 1], [[0, 2 * NX]], base=0, channel_multiplier=0).then_inc(S["entry_iota"], 1)
        pool.wait_ge(S["entry_iota"], 3)
        table_dram = slot_table.rearrange("(g p) w -> p g w", p=P)
        pool.dma_start(table_dram, table[:, :, :]).then_inc(S["table_preset"], 16)
        pool.wait_ge(S["table_preset"], 16)
        pool.wait_ge(S["dest_made"], 1)
        pool.wait_ge(S["entry_made"], 1)
        for i in range(NT):
            for j in range(2):
                nc.gpsimd.indirect_dma_start(
                    slot_table, bass.IndirectOffsetOnAxis(ap=dest[:, j, i:i + 1], axis=0), entry[:, i, j, :],
                    None).then_inc(S["table_filled"], 16)
        pool.wait_ge(S["table_filled"], 16 * 2 * NT)
        pool.dma_start(table[:, :, :], table_dram).then_inc(S["table_landed"], 16)
        pool.wait_ge(S["table_landed"], 16)

        def fetch(s, k, p):
            if not peeled(s) or s >= 2:
                pool.wait_ge(S["add_done"], 32 * (s - 1))
                pool.wait_ge(S["turned"], 2 * (s - 1))
            nc.gpsimd.tensor_copy(slots[p][:, :, :], table[:, bass.ts(s, 2), :]).then_inc(S["slots_made"], 1)
            pool.wait_ge(S["slots_made"], s + 1)
            pool.sem_inc(S["gather_passed"], 1)
            for j in range(2):
                nc.gpsimd.indirect_dma_start(
                    x_rows[p][j][:, :], None, xn,
                    bass.IndirectOffsetOnAxis(ap=slots[p][:, j, 0:1], axis=0)).then_inc(x_landed[p], 16)

        def add(s, p):
            for j in range(2):
                pool.wait_ge(S["y_taken"], 2 * (NS + s) + j + 1)
                if j or not peeled(s) or s:
                    pool.wait_ge(S["add_done"], 16 * (2 * s + j))
                pool.sem_inc(S["gather_passed"], 1)
                nc.gpsimd.indirect_dma_start(
                    out, bass.IndirectOffsetOnAxis(ap=slots[p][:, j, 0:1], axis=0), y_sb[j][:, :], None,
                    compute_op=ALU.add).then_inc(S["add_done"], 16)

        fetch(0, 0, 0)
        fetch(1, 0, 1)
        pool.wait_ge(S["out_stored"], 16 * 2 * NS)
        for s in range(2):
            add(s, s)
            fetch(s + 2, 1, s)
        with pool.Fori(1, (NX - 3) // 2) as k:
            for p in range(2):
                add(k * 2 + p, p)
                fetch(k * 2 + (2 + p), k + 1, p)
        for s in range(NX - 3, NX):
            add(s, s % 2)
            if s + 2 < NX:
                fetch(s + 2, (s + 2) // 2, s % 2)
        pool.wait_ge(S["add_done"], 32 * NX)

    @block.scalar
    def _(act):
        def split_x(G, j, s=None):
            if not peeled(G) or G:
                act.wait_ge(S["hu_ready"], 3 * G)
            if s is None:
                source = xt[:, :, bass.ds(G * GROUP + j * P, P)]
            else:
                act.wait_ge(S["turned"], 2 * s + j + 1)
                source = ps_x[j][:, :, :]
            nc.scalar.activation(x_hi[:, :, bass.ts(j, P)], source, ACT.Copy).then_inc(S["xhi_made"], 1)

        def gate(G, m):
            act.wait_ge(S["hu_ready"], 3 * G + m + 1)
            nc.scalar.activation(silu[0:HR[m], m, :], ps_h[m][0:HR[m], 0, :], ACT.Silu).then_inc(S["silu_made"], 1)

        def weight_y(G, s, p):
            for j in range(2):
                act.wait_ge(S["y_ready"], 2 * G + j + 1)
                act.wait_ge(S["slots_made"], s + 1)
                if not peeled(s) or s:
                    act.wait_ge(S["add_done"], 16 * (2 * s - 1 + j))
                nc.scalar.activation(y_sb[j][:, :], ps_y[j][:, :], ACT.Copy,
                                     scale=slots[p][:, j, 1:2].bitcast(F32)).then_inc(S["y_taken"], 1)

        def split_w(k, p, part, free):
            if free is not None:
                act.wait_ge(S["y_ready"], free)
            if part == 0:
                act.wait_ge(S["w1_landed"], 16 * (k + 1))
                nc.scalar.activation(w1_hi[p][:, :, :], w1_f[:, :, :], ACT.Copy).then_inc(S["whi_made"], 1)
            elif part == 1:
                act.wait_ge(S["w3_landed"], 16 * (k + 1))
                nc.scalar.activation(w3_hi[p][:, :, :], w3_f[:, :, :], ACT.Copy).then_inc(S["whi_made"], 1)
            else:
                act.wait_ge(S["w2_landed"], 32 * (k + 1))
                nc.scalar.activation(w2_hi[p][:, 0:MH - 1, :], w2_f[:, 0:MH - 1, :],
                                     ACT.Copy).then_inc(S["whi_made"], 1)
                nc.scalar.activation(w2_hi[p][0:HR[-1], MH - 1, :], w2_f[0:HR[-1], MH - 1, :],
                                     ACT.Copy).then_inc(S["whi_made"], 1)

        act.wait_ge(S["gate_turned"], 1)
        nc.scalar.activation(gate_t[:, :, :], ps_r[:, 0, 0:KC * E].rearrange("p (c e) -> p c e", e=E),
                             ACT.Copy).then_inc(S["gate_made"], 1)
        for q in range(T // L):
            act.wait_ge(S["logits_ready"], q + 1)
            nc.scalar.activation(logits_t[:, bass.ts(q, L)], ps_y[q % 2][0:E, :], ACT.Copy).then_inc(S["logits_made"], 1)
        act.wait_ge(S["logits_turned"], 1)
        nc.scalar.activation(e_neg[:, :, :], ps_r[:, 0, :].rearrange("p (i e) -> p i e", e=E), ACT.Exp,
                             scale=-1.0).then_inc(S["exp_made"], 1)
        for part in range(3):
            split_w(0, 0, part, None)
        split_x(0, 0)
        split_x(0, 1)

        def shared_step(G):
            for m in range(MH):
                gate(G, m)
            split_x(G + 1, 0)
            split_x(G + 1, 1)

        with act.Fori(0, NS - 1) as G:
            shared_step(G)
        for m in range(MH):
            gate(NS - 1, m)
            split_w(1, 1, m, None)
        split_x(NS, 0, 0)
        split_x(NS, 1, 0)

        def expert_step(s, p):
            G = s + NS
            for m in range(MH):
                split_w(s + 2, p, m, 2 * G)
                gate(G, m)
            split_x(G + 1, 0, s + 1)
            split_x(G + 1, 1, s + 1)
            weight_y(G, s, p)

        for s in range(2):
            expert_step(s, s)
        with act.Fori(1, (NX - 1) // 2) as k:
            for p in range(2):
                expert_step(k * 2 + p, p)
        for m in range(MH):
            gate(NS + NX - 1, m)
        weight_y(NS + NX - 1, NX - 1, (NX - 1) % 2)

    @block.vector
    def _(dve):
        def split_x(G, j, s=None):
            dve.wait_ge(S["xhi_made"], 2 * G + j + 1)
            source = xt[:, :, bass.ds(G * GROUP + j * P, P)] if s is None else ps_x[j][:, :, :]
            nc.vector.tensor_tensor(x_lo[:, :, bass.ts(j, P)], source, x_hi[:, :, bass.ts(j, P)].bitcast(F32),
                                    ALU.subtract).then_inc(S["xlo_made"], 1)

        def hidden(G, m):
            r = HR[m]
            dve.wait_ge(S["silu_made"], 3 * G + m + 1)
            nc.vector.tensor_tensor(g_f[0:r, m, :], silu[0:r, m, :], ps_h[m][0:r, 1, :],
                                    ALU.mult).then_inc(S["gf_made"], 1)
            dve.wait_ge(S["gf_made"], 3 * G + m + 1)
            if not peeled(G) or G:
                dve.wait_ge(S["y_ready"], 2 * G)
            nc.vector.tensor_copy(g_hi[0:r, m, :], g_f[0:r, m, :]).then_inc(S["ghi_made"], 1)
            dve.wait_ge(S["ghi_made"], 3 * G + m + 1)
            nc.vector.tensor_tensor(g_lo[0:r, m, :], g_f[0:r, m, :], g_hi[0:r, m, :].bitcast(F32),
                                    ALU.subtract).then_inc(S["glo_made"], 1)

        def add_x1(G):
            for j in range(2):
                dve.wait_ge(S["y_ready"], 2 * G + j + 1)
                t = G * 2 + j
                nc.vector.tensor_tensor(x1[:, t, :], ps_y[j][:, :], x1[:, t, :], ALU.add).then_inc(S["y_taken"], 1)

        def split_w(k, p, part):
            dve.wait_ge(S["whi_made"], 4 * k + part + 1)
            if part < 2:
                f, hi, lo = ((w1_f, w1_hi[p], w1_lo[p]), (w3_f, w3_hi[p], w3_lo[p]))[part]
                nc.vector.tensor_tensor(lo[:, :, :], f[:, :, :], hi[:, :, :].bitcast(F32),
                                        ALU.subtract).then_inc(S["wlo_made"], 1)
                return
            nc.vector.tensor_tensor(w2_lo[p][:, 0:MH - 1, :], w2_f[:, 0:MH - 1, :],
                                    w2_hi[p][:, 0:MH - 1, :].bitcast(F32), ALU.subtract).then_inc(S["wlo_made"], 1)
            dve.wait_ge(S["whi_made"], 4 * k + 4)
            r = HR[-1]
            nc.vector.tensor_tensor(w2_lo[p][0:r, MH - 1, :], w2_f[0:r, MH - 1, :],
                                    w2_hi[p][0:r, MH - 1, :].bitcast(F32), ALU.subtract).then_inc(S["wlo_made"], 1)

        nc.vector.memset(ones_b[:, :], 1.0).then_inc(S["consts_set"], 1)
        for part in range(3):
            split_w(0, 0, part)
        split_x(0, 0)
        split_x(0, 1)

        dve.wait_ge(S["exp_made"], 1)
        nc.vector.tensor_scalar(e_one[:, :, :], e_neg[:, :, :], 1.0, None, ALU.add).then_inc(S["score_step"], 1)
        dve.wait_ge(S["score_step"], 1)
        nc.vector.reciprocal(score[:, :, :], e_one[:, :, :]).then_inc(S["score_step"], 1)
        dve.wait_ge(S["score_step"], 2)
        for i in range(NT):
            nc.vector.max(top[:, i, :], score[:, i, :]).then_inc(S["top_made"], 1)
        for i in range(NT):
            dve.wait_ge(S["top_made"], i + 1)
            last = nc.vector.max_index(top_i[:, i, :], top[:, i, :], score[:, i, :])
        last.then_inc(S["score_step"], 1)
        dve.wait_ge(S["score_step"], 3)
        nc.vector.tensor_copy(top_f[:, :, :], top_i[:, :, 0:2]).then_inc(S["score_step"], 1)
        dve.wait_ge(S["score_step"], 4)
        dve.wait_ge(S["iota_made"], 2)
        for j in range(2):
            nc.vector.tensor_tensor(chosen[j][:, :, :], iota_e[:, :].unsqueeze(1).to_broadcast([P, NT, E]),
                                    top_f[:, :, j:j + 1].to_broadcast([P, NT, E]),
                                    ALU.is_equal).then_inc(S["score_step"], 1)
        dve.wait_ge(S["score_step"], 6)
        nc.vector.tensor_tensor(either[:, :, :], chosen[0][:, :, :], chosen[1][:, :, :],
                                ALU.add).then_inc(S["either_made"], 1)
        nc.vector.tensor_tensor(top_sum[:, :], top[:, :, 0], top[:, :, 1], ALU.add).then_inc(S["score_step"], 1)
        dve.wait_ge(S["score_step"], 7)
        nc.vector.tensor_scalar(top_sum[:, :], top_sum[:, :], 1e-20, None, ALU.add).then_inc(S["score_step"], 1)
        dve.wait_ge(S["score_step"], 8)
        nc.vector.reciprocal(top_inv[:, :], top_sum[:, :]).then_inc(S["score_step"], 1)
        dve.wait_ge(S["score_step"], 9)
        for j in range(2):
            nc.vector.scalar_tensor_tensor(entry[:, :, j, 1].bitcast(F32), top[:, :, j], dims["routed_scale"],
                                           top_inv[:, :], ALU.mult, ALU.mult).then_inc(S["score_step"], 1)
        dve.wait_ge(S["score_step"], 11)
        dve.wait_ge(S["entry_iota"], 3)
        dve.sem_inc(S["entry_made"], 1)

        ranks = ps_r[:, 1, :].rearrange("p (e i) -> p e i", e=E)
        totals = ps_r[:, 2, :]
        steps = [0]

        def routed(ins):
            steps[0] += 1
            ins.then_inc(S["route_step"], 1)
            dve.wait_ge(S["route_step"], steps[0])

        dve.wait_ge(S["ranks_ready"], 1)
        routed(nc.vector.tensor_tensor_scan(running[:, :, :].rearrange("p e i -> p (e i)"), ones_f[:, 0:E * NT], totals,
                                            0.0, ALU.mult, ALU.add))
        routed(nc.vector.memset(before[:, 0:1], 0.0))
        routed(nc.vector.tensor_copy(before[:, 1:E], running[:, 0:E - 1, NT - 1]))
        routed(nc.vector.tensor_tensor(count[:, :], running[:, :, NT - 1], before[:, :], ALU.subtract))
        routed(nc.vector.tensor_scalar(need[:, :], count[:, :], 1.0 / GROUP, 0.5 - 0.5 / GROUP, ALU.mult, ALU.add))
        routed(nc.vector.tensor_scalar(need_up[:, :], need[:, :], 8388608.0, None, ALU.add))
        routed(nc.vector.tensor_scalar(need[:, :], need_up[:, :], -8388608.0, None, ALU.add))
        routed(nc.vector.tensor_tensor_scan(ends[:, :], ones_f[:, 0:E], need[:, :], 0.0, ALU.mult, ALU.add))
        routed(nc.vector.tensor_tensor(past[:, :, :], ends[0:1, :].unsqueeze(1).to_broadcast([1, NX + 1, E]),
                                       iota_g[:, :].unsqueeze(2).to_broadcast([1, NX + 1, E]), ALU.is_le))
        routed(nc.vector.tensor_reduce(group_f[:, :], past[:, :, :], AX.X, ALU.add))
        nc.vector.tensor_scalar(group_e[:, :], group_f[:, :], float(E - 1), None, ALU.min).then_inc(S["group_made"], 1)
        routed(nc.vector.tensor_tensor(starts[:, :], ends[:, :], need[:, :], ALU.subtract))
        routed(nc.vector.scalar_tensor_tensor(starts[:, :], starts[:, :], float(GROUP), before[:, :], ALU.mult,
                                              ALU.subtract))
        routed(nc.vector.tensor_tensor(place_a[:, :, :].rearrange("p e i -> p (e i)"),
                                       running[:, :, :].rearrange("p e i -> p (e i)"), totals, ALU.subtract))
        routed(nc.vector.tensor_tensor(place_b[:, :, :], place_a[:, :, :], ranks, ALU.add))
        routed(nc.vector.tensor_tensor(place_c[:, :, :], place_b[:, :, :],
                                       starts[:, :].unsqueeze(2).to_broadcast([P, E, NT]), ALU.add))
        for j in range(2):
            routed(nc.vector.tensor_tensor(picked[j][:, :, :], chosen[j][:, :, :],
                                           place_c[:, :, :].rearrange("p e i -> p i e"), ALU.mult))
            routed(nc.vector.tensor_reduce(dest_f[:, j, :], picked[j][:, :, :], AX.X, ALU.add))
        nc.vector.tensor_copy(dest[:, :, :], dest_f[:, :, :]).then_inc(S["dest_made"], 1)

        def shared_step(G):
            for m in range(MH):
                hidden(G, m)
            split_x(G + 1, 0)
            split_x(G + 1, 1)
            add_x1(G)

        shared_step(0)
        with dve.Fori(1, NS - 1) as G:
            shared_step(G)
        for m in range(MH):
            hidden(NS - 1, m)
            split_w(1, 1, m)
        add_x1(NS - 1)
        split_x(NS, 0, 0)
        split_x(NS, 1, 0)

        def expert_step(s, p):
            G = s + NS
            for m in range(MH):
                split_w(s + 2, p, m)
                hidden(G, m)
            split_x(G + 1, 0, s + 1)
            split_x(G + 1, 1, s + 1)

        with dve.Fori(0, (NX - 1) // 2) as k:
            for p in range(2):
                expert_step(k * 2 + p, p)
        for m in range(MH):
            hidden(NS + NX - 1, m)

    @block.tensor
    def _(pe):
        def up(G, k, p):
            pe.wait_ge(S["xlo_made"], 2 * G + 2)
            pe.wait_ge(S["wlo_made"], 4 * k + 2)
            for m in range(MH):
                cols = slice(m * P, m * P + HR[m])
                if not peeled(G) or G:
                    pe.wait_ge(S["gf_made"], 3 * G + m - 2)
                for half, (hi, lo) in enumerate(((w1_hi, w1_lo), (w3_hi, w3_lo))):
                    acc = ps_h[m][0:HR[m], half, :]
                    for c in range(KC):
                        nc.tensor.matmul(acc, hi[p][:, c, cols], x_hi[:, c, :], start=c == 0, stop=False)
                        nc.tensor.matmul(acc, hi[p][:, c, cols], x_lo[:, c, :], start=False, stop=False)
                        last = nc.tensor.matmul(acc, lo[p][:, c, cols], x_hi[:, c, :], start=False, stop=c == KC - 1)
                last.then_inc(S["hu_ready"], 1)

        def down(G, k, p):
            pe.wait_ge(S["wlo_made"], 4 * k + 4)
            for j in range(2):
                if not peeled(G) or G:
                    pe.wait_ge(S["y_taken"], 2 * G + j - 1)
                else:
                    pe.wait_ge(S["logits_made"], T // L)
                for m in range(MH):
                    pe.wait_ge(S["glo_made"], 3 * G + m + 1)
                    r, tokens = HR[m], bass.ts(j, P)
                    nc.tensor.matmul(ps_y[j][:, :], g_hi[0:r, m, tokens], w2_hi[p][0:r, m, :], start=m == 0, stop=False)
                    nc.tensor.matmul(ps_y[j][:, :], g_hi[0:r, m, tokens], w2_lo[p][0:r, m, :], start=False, stop=False)
                    last = nc.tensor.matmul(ps_y[j][:, :], g_lo[0:r, m, tokens], w2_hi[p][0:r, m, :], start=False,
                                            stop=m == MH - 1)
                last.then_inc(S["y_ready"], 1)

        def turn(s, k, p):
            pe.wait_ge(x_landed[p], 32 * (k + 1))
            for j in range(2):
                if not peeled(s) or s:
                    pe.wait_ge(S["xlo_made"], 2 * (s + NS) + j - 1)
                for c in range(KC):
                    last = nc.tensor.transpose(ps_x[j][:, c, :], x_rows[p][j][:, bass.ts(c, P)], ident[:, :])
                last.then_inc(S["turned"], 1)

        pe.wait_ge(S["gate_landed"], 16)
        for c in range(KC):
            last = nc.tensor.transpose(ps_r[:, 0, c * E:(c + 1) * E], gate_sb[:, bass.ts(c, P)], ident[0:E, 0:E])
        last.then_inc(S["gate_turned"], 1)
        pe.wait_ge(S["gate_made"], 1)
        for q in range(T // L):
            if q >= 2:
                pe.wait_ge(S["logits_made"], q - 1)
            for c in range(KC):
                last = nc.tensor.matmul(ps_y[q % 2][0:E, :], gate_t[:, c, :], xt[:, c, bass.ts(q, L)], start=c == 0,
                                        stop=c == KC - 1)
            last.then_inc(S["logits_ready"], 1)
        pe.wait_ge(S["logits_made"], T // L)
        for i in range(NT):
            last = nc.tensor.transpose(ps_r[:, 0, i * E:(i + 1) * E], logits_t[:, bass.ts(i, P)], ident[0:E, 0:E])
        last.then_inc(S["logits_turned"], 1)
        up(0, 0, 0)
        pe.wait_ge(S["either_made"], 1)
        pe.wait_ge(S["upper_made"], 1)
        by_expert = either[:, :, :].rearrange("p i e -> p e i")
        nc.tensor.matmul(ps_r[:, 1, :], upper[:, :], by_expert, start=True, stop=True)
        nc.tensor.matmul(ps_r[:, 2, :], ones_b[:, :], by_expert, start=True, stop=True).then_inc(S["ranks_ready"], 1)
        down(0, 0, 0)
        with pe.Fori(1, NS) as G:
            up(G, 0, 0)
            down(G, 0, 0)
        turn(0, 0, 0)
        with pe.Fori(0, (NX - 1) // 2) as k:
            for p in range(2):
                s = k * 2 + p
                up(s + NS, s + 1, 1 - p)
                turn(k * 2 + (p + 1), k + p, 1 - p)
                down(s + NS, s + 1, 1 - p)
        up(NS + NX - 1, NX, NX % 2)
        down(NS + NX - 1, NX, NX % 2)


def build(nc, ins, out):
    x = ins["x"]
    B, C, L = x.shape
    E, _, H = ins["L0_ffn_w1"].shape
    T = B * C
    NT = T // P
    NX = 2 * T // (2 * P) + E - 1
    dims = {"B": B, "C": C, "L": L, "T": T, "E": E, "H": H, "routed_scale": 2.5}
    dram = {
        "x": x, "ctx": ins["ctx_2048"], "lengths": ins["itok_B_779_1933"], "out": out,
        "gate": ins["L0_ffn_gate_w"], "w1": ins["L0_ffn_w1"], "w2": ins["L0_ffn_w2"], "w3": ins["L0_ffn_w3"],
        "sw1": ins["L0_ffn_sw1"], "sw2": ins["L0_ffn_sw2"], "sw3": ins["L0_ffn_sw3"],
        "xn": nc.dram_tensor("xn", (T + P, L), F32, kind="Internal").ap(),
        "slots": nc.dram_tensor("slots", (NX * 2 * P, 2), U32, kind="Internal").ap(),
    }
    with ExitStack() as common:
        def sb(name, shape):
            return common.enter_context(nc.sbuf_tensor(name, shape, F32))

        keep = {"x1": sb("x1", [P, NT, L]), "xt": sb("xt", [P, L // P, T]), "ident": sb("ident", [P, P]),
                "ones_f": sb("ones_f", [P, P])}
        for stage in (attention_block, experts_block):
            with ExitStack() as ctx:
                stage(nc, ctx, dims, dram, keep)


_INS = ['x', 'ctx_2048', 'itok_B_779_1933', 'L0_ffn_gate_w', 'L0_ffn_w1', 'L0_ffn_w2', 'L0_ffn_w3', 'L0_ffn_sw1',
        'L0_ffn_sw2', 'L0_ffn_sw3']


def kernel(**inputs):
    import concourse.bacc as _bacc
    from concourse.bass_utils import run_bass_kernel_spmd as _run

    nc = _bacc.Bacc("TRN2", target_bir_lowering=False, num_devices=1)
    arrays, aps = {}, {}
    for name in _INS:
        a = np.ascontiguousarray(inputs[name])
        arrays[f"in_{name}_dram"] = a
        aps[name] = nc.dram_tensor(f"in_{name}_dram", a.shape, mybir.dt.from_np(a.dtype), kind="ExternalInput").ap()
    shape = inputs["x"].shape
    rows = shape[0] * shape[1]
    out = nc.dram_tensor("out_0_dram", (rows + P, shape[2]), F32, kind="ExternalOutput").ap()
    build(nc, aps, out)
    r = _run(nc, [arrays], core_ids=[0])
    return r.results[0]["out_0_dram"][:rows].reshape(shape)
```

```python
from contextlib import ExitStack

import numpy as np

import concourse.bass as bass
from concourse import mybir

ALU = mybir.AluOpType
ACT = mybir.ActivationFunctionType
AX = mybir.AxisListType
F32 = mybir.dt.float32
F32R = mybir.dt.float32r
BF16 = mybir.dt.bfloat16
I32 = mybir.dt.int32
U32 = mybir.dt.uint32

P = 128
EPS = 1e-5
HEADS = 8
DH = 64
SCALE = 1.0 / (DH ** 0.5 * float(np.log(20)))


def part_sum(part):
    return 32 if part == 2 else 16


def load_part(sp, weights, part, w, landed):
    f = weights["f"][part]
    if part < 2:
        sp.dma_start(f[:, :, :], w.rearrange("(c p) h -> p c h", p=P)).then_inc(landed, 16)
        return
    m = f.shape[1] - 1
    rows = w.shape[0]
    sp.dma_start(f[:, 0:m, :], w[0:m * P].rearrange("(m p) n -> p m n", p=P)).then_inc(landed, 16)
    sp.dma_start(f[0:rows - m * P, m, :], w[m * P:rows]).then_inc(landed, 16)


def split_high(nc, weights, part, p, made):
    f, hi = weights["f"][part], weights["hi"][p][part]
    if part < 2:
        nc.scalar.activation(hi[:, :, :], f[:, :, :], ACT.Copy).then_inc(made, 1)
        return
    m, r = f.shape[1] - 1, weights["last_rows"]
    nc.scalar.activation(hi[:, 0:m, :], f[:, 0:m, :], ACT.Copy).then_inc(made, 1)
    nc.scalar.activation(hi[0:r, m, :], f[0:r, m, :], ACT.Copy).then_inc(made, 1)


def split_low(nc, weights, part, p, made):
    f, hi, lo = weights["f"][part], weights["hi"][p][part], weights["lo"][p][part]
    if part < 2:
        nc.vector.tensor_tensor(lo[:, :, :], f[:, :, :], hi[:, :, :].bitcast(F32), ALU.subtract).then_inc(made, 1)
        return
    m, r = f.shape[1] - 1, weights["last_rows"]
    nc.vector.tensor_tensor(lo[:, 0:m, :], f[:, 0:m, :], hi[:, 0:m, :].bitcast(F32), ALU.subtract).then_inc(made, 1)
    nc.vector.tensor_tensor(lo[0:r, m, :], f[0:r, m, :], hi[0:r, m, :].bitcast(F32), ALU.subtract).then_inc(made, 1)


def attention_block(nc, ctx, dims, dram, keep):
    B, C, L = dims["B"], dims["C"], dims["L"]
    NH = B * HEADS
    NT = B * C // P
    KC = L // P

    def sb(name, shape, dt=F32):
        return ctx.enter_context(nc.sbuf_tensor(name, shape, dt))

    def sem(name):
        return ctx.enter_context(nc.semaphore(name))

    x1, xt = keep["x1"], keep["xt"]
    ident, ones_f = keep["ident"], keep["ones_f"]
    gate_t, logits_t, weights = keep["gate_t"], keep["logits_t"], keep["weights"]
    E, H = dims["E"], dims["H"]

    xd = [sb(f"xd{p}", [P, L]) for p in range(2)]
    kd = [sb(f"kd{p}", [P, L]) for p in range(2)]
    k_rows = [sb(f"k_rows{p}", [P, L]) for p in range(2)]
    q_f = sb("q_f", [DH, L])
    q_hi = [sb(f"q_hi{p}", [P, L], F32R) for p in range(2)]
    q_lo = [sb(f"q_lo{p}", [P, L], F32R) for p in range(2)]
    k_hl = [sb(f"k_hl{p}", [P, L], F32R) for p in range(2)]
    k_h1 = [sb(f"k_h1{p}", [P, L], F32R) for p in range(2)]
    v_t = [sb(f"v_t{p}", [P, KC, 3, DH]) for p in range(2)]
    probs = [sb(f"probs{p}", [P, KC, L]) for p in range(2)]
    diag = sb("diag", [P, KC, P], F32R)
    numer = sb("numer", [P, L])
    sums_t = sb("sums_t", [P, L])
    recip_col = sb("recip_col", [P, L // 32])
    recip = sb("recip", [P, L])
    attn = sb("attn", [P, L])
    x_hat = [sb(f"x_hat{p}", [P, L]) for p in range(2)]
    gate_sb = sb("gate_sb", [E, L])
    neg_ident = sb("neg_ident", [P, P])
    ones_r = sb("ones_r", [P, P], F32R)
    zeros_f = sb("zeros_f", [P, L])
    stats = [sb(f"stats{p}", [P, 6]) for p in range(2)]
    mv = [sb(f"mv{p}", [P, 2]) for p in range(2)]
    rstd = [sb(f"rstd{p}", [P, 2]) for p in range(2)]
    var_e = sb("var_e", [P, 1])
    minus_half = sb("minus_half", [P, 1])
    stats2 = sb("stats2", [P, 6])
    mv2 = sb("mv2", [P, 2])
    rstd2 = sb("rstd2", [P, 2])
    qmax = [sb(f"qmax{p}", [P, KC]) for p in range(2)]
    len_i = sb("len_i", [P, B], I32)
    len_f = sb("len_f", [P, B])
    len_ln = sb("len_ln", [P, B])
    s_pair = sb("s_pair", [P, NH // 2])

    ps_max = ctx.enter_context(nc.psum_tensor("ps_max", [P, 2, L], F32))
    ps_s = ctx.enter_context(nc.psum_tensor("ps_s", [P, KC, L], F32))
    ps_o = ctx.enter_context(nc.psum_tensor("ps_o", [P, L], F32))
    ps_t = ctx.enter_context(nc.psum_tensor("ps_t", [P, KC, P], F32))

    len_landed = sem("len_landed")
    x1_landed = sem("x1_landed")
    x_landed = [sem(f"x_landed{p}") for p in range(2)]
    k_landed = [sem(f"k_landed{p}") for p in range(2)]
    rows_landed = [sem(f"k_rows_landed{p}") for p in range(2)]
    pad_stored = sem("pad_stored")
    ident_zero = sem("ident_zero")
    ident_made = sem("ident_made")
    consts_made = sem("consts_made")
    len_cast = sem("len_cast")
    len_logged = sem("len_logged")
    scale_made = sem("scale_made")
    stats_raw = sem("stats_raw")
    stats_made = sem("stats_made")
    rstd_step = sem("rstd_step")
    rstd_made = sem("rstd_made")
    qhi_made = sem("qhi_made")
    khi_made = sem("khi_made")
    kh1_made = sem("kh1_made")
    qf_made = sem("qf_made")
    qlo_made = sem("qlo_made")
    klo_made = sem("klo_made")
    max_ready = sem("max_ready")
    max_taken = sem("max_taken")
    diag_made = sem("diag_made")
    row_ready = sem("row_ready")
    row_made = sem("row_made")
    vt_ready = sem("vt_ready")
    v_made = sem("v_made")
    s_ready = sem("s_ready")
    exp_done = sem("exp_done")
    pv_done = sem("pv_done")
    numer_made = sem("numer_made")
    sums_turned = sem("sums_turned")
    recip_made = sem("recip_made")
    attn_made = sem("attn_made")
    x1_made = sem("x1_made")
    stats2_raw = sem("stats2_raw")
    stats2_made = sem("stats2_made")
    rstd2_made = sem("rstd2_made")
    xhat_made = sem("xhat_made")
    xhat_stored = sem("xhat_stored")
    xt_ready = sem("xt_ready")
    xt_made = sem("xt_made")
    gate_landed = sem("gate_landed")
    gate_turned = sem("gate_turned")
    gate_made = sem("gate_made")
    logits_ready = sem("logits_ready")
    logits_made = sem("logits_made")
    w_landed = [sem(f"shared_w{n}_landed") for n in (1, 3, 2)]
    whi_made = sem("shared_whi_made")
    wlo_made = sem("shared_wlo_made")
    pool_passed, act_passed, dve_passed, sp_passed = (sem(f"{e}_passed") for e in ("pool", "act", "dve", "sp"))

    x_rows = dram["x"].rearrange("b (h d) l -> (b h) d l", d=DH)
    c_rows = dram["ctx"].rearrange("b (h d) l -> (b h) d l", d=DH)
    xn_rows = dram["xn"]
    k_pairs = dram["ctx"].rearrange("b (i p) l -> (b i) p l", p=P)
    head_rows = [slice(0, DH), slice(DH, P)]

    def within(i, p, ahead=0):
        return not isinstance(i, int) or 0 <= 2 * i + p + ahead < NH

    block = ctx.enter_context(nc.Block("attention"))

    @block.sync
    def _(sp):
        def load(i, b):
            if not isinstance(i, int) or i >= 2:
                pairs = i - 1 if isinstance(i, int) else sp.snap(i - 1)
                sp.wait_ge(vt_ready, pairs)
                sp.sem_inc(sp_passed, 1)
            sp.dma_start(k_rows[b][:, :], k_pairs[i]).then_inc(rows_landed[b], 16)
            for p in range(2):
                if not isinstance(i, int) or i >= 1:
                    heads = 2 * i + (p - 1)
                    if not isinstance(i, int):
                        heads = sp.snap(heads)
                    sp.wait_ge(klo_made, heads)
                    sp.wait_ge(kh1_made, heads)
                    sp.wait_ge(qlo_made, heads)
                    sp.sem_inc(sp_passed, 1)
                for half in head_rows:
                    sp.dma_start(xd[p][half, :], x_rows[2 * i + p]).then_inc(x_landed[p], 16)
                for half in head_rows:
                    sp.dma_start(kd[p][half, :], c_rows[2 * i + p]).then_inc(k_landed[p], 16)

        def store(t, b):
            sp.wait_ge(xhat_made, t + 1)
            sp.dma_start(xn_rows[bass.ts(t, P), :], x_hat[b][:, :]).then_inc(xhat_stored, 16)

        load(0, 0)
        sp.dma_start(len_i[:, :], dram["lengths"].partition_broadcast(P)).then_inc(len_landed, 16)
        sp.dma_start(gate_sb[:, :], dram["gate"]).then_inc(gate_landed, 16)
        load(1, 1)
        sp.dma_start(x1[:, :, :], dram["x"].rearrange("b (t p) l -> p (b t) l", p=P)).then_inc(x1_landed, 16)
        sp.wait_ge(consts_made, 1)
        sp.dma_start(xn_rows[NT * P:NT * P + P, :], zeros_f[:, :]).then_inc(pad_stored, 16)
        sp.dma_start(dram["out"][NT * P:NT * P + P, :], zeros_f[:, :]).then_inc(pad_stored, 16)
        load(2, 0)
        load(3, 1)
        for n, w in enumerate((dram["sw1"], dram["sw3"], dram["sw2"])):
            load_part(sp, weights, n, w, w_landed[n])
        with sp.Fori(0, (NT - 4) // 2) as k:
            for b in range(2):
                load(k * 2 + (4 + b), b)
                store(k * 2 + b, b)
        for t in range(NT - 4, NT):
            store(t, t % 2)
        sp.wait_ge(xhat_stored, 16 * NT)
        sp.wait_ge(pad_stored, 32)

    @block.gpsimd
    def _(pool):
        nc.gpsimd.memset(ident[:, :], 0.0).then_inc(ident_zero, 1)
        pool.wait_ge(ident_zero, 1)
        nc.gpsimd.affine_select(out=ident[:, :], in_=ident[:, :], compare_op=ALU.not_equal, fill=1.0, base=0,
                                pattern=[[-1, P]], channel_multiplier=1).then_inc(ident_made, 1)
        nc.gpsimd.memset(minus_half[:, :], -0.5).then_inc(ident_zero, 1)
        pool.wait_ge(ident_zero, 2)

        def inverse_sigma(made, count, mean_var, out):
            nc.gpsimd.tensor_scalar(var_e[:, :], mean_var[:, 1:2], EPS, None, ALU.add).then_inc(rstd_step, 1)
            pool.wait_ge(rstd_step, count * 2 + 1)
            nc.gpsimd.tensor_tensor(out[:, 0:1], var_e[:, :], minus_half[:, :], ALU.pow).then_inc(rstd_step, 1)
            pool.wait_ge(rstd_step, count * 2 + 2)
            pool.sem_inc(pool_passed, 1)
            nc.gpsimd.tensor_scalar(out[:, 1:2], mean_var[:, 0:1], out[:, 0:1], -1.0, ALU.mult,
                                    ALU.mult).then_inc(made, 1)

        def queries(i, p, calls):
            pool.wait_ge(stats_made, 2 * i + p + 1)
            pool.sem_inc(pool_passed, 1)
            inverse_sigma(rstd_made, calls, mv[p], rstd[p])
            pool.wait_ge(rstd_made, 2 * i + p + 1)
            pool.sem_inc(pool_passed, 1)
            nc.gpsimd.tensor_scalar(q_f[:, :], xd[p][0:DH, :], rstd[p][0:DH, 0:1], rstd[p][0:DH, 1:2], ALU.mult,
                                    ALU.add).then_inc(qf_made, 1)
            pool.wait_ge(qhi_made, 2 * i + p + 1)
            pool.wait_ge(qf_made, 2 * i + p + 1)
            nc.gpsimd.tensor_tensor(q_lo[p][0:DH, :], q_f[:, :], q_hi[p][0:DH, :].bitcast(F32),
                                    ALU.subtract).then_inc(qlo_made, 1)
            pool.wait_ge(qlo_made, 2 * i + p + 1)
            pool.sem_inc(pool_passed, 1)

        def add_attention(i):
            pool.wait_ge(attn_made, i + 1)
            nc.gpsimd.tensor_tensor(x1[:, i, :], x1[:, i, :], attn[:, :], ALU.add).then_inc(x1_made, 1)
            pool.wait_ge(x1_made, i + 1)
            pool.sem_inc(pool_passed, 1)

        def tile_sigma(t, calls):
            pool.wait_ge(stats2_made, t + 1)
            pool.sem_inc(pool_passed, 1)
            inverse_sigma(rstd2_made, calls, mv2, rstd2)

        for n in range(3):
            queries(n // 2, n % 2, n)
        pool.wait_ge(x1_landed, 16)

        def pair(i, calls):
            later = within(i, 0, 3)
            if later:
                queries(i + 1, 1, calls)
            if not isinstance(i, int) or i >= 1:
                add_attention(i - 1)
            if within(i, 0, 4):
                queries(i + 2, 0, calls + 1)
            if not isinstance(i, int) or i >= 1:
                tile_sigma(i - 1, calls + 2 if within(i, 0, 4) else calls + 1 if later else calls)

        pair(0, 3)
        with pool.Fori(1, NT - 2) as i:
            pair(i, i * 3 + 2)
        calls = (NT - 2) * 3 + 2
        pair(NT - 2, calls)
        pair(NT - 1, calls + 2)
        add_attention(NT - 1)
        tile_sigma(NT - 1, calls + 3)

    @block.scalar
    def _(act):
        act.wait_ge(len_cast, 1)
        nc.scalar.activation(len_ln[:, :], len_f[:, :], ACT.Ln).then_inc(len_logged, 1)

        def highs(i, p):
            act.wait_ge(k_landed[p], 32 * (i + 1))
            if not isinstance(i, int) or i >= 1:
                act.wait_ge(s_ready, 2 * (2 * i + p - 1))
            nc.scalar.activation(k_hl[p][:, :], kd[p][:, :], ACT.Copy).then_inc(khi_made, 1)
            act.wait_ge(rstd_made, 2 * i + p + 1)
            act.wait_ge(x_landed[p], 32 * (i + 1))
            nc.scalar.activation(q_hi[p][:, :], xd[p][:, :], ACT.Identity, scale=rstd[p][:, 0:1],
                                 bias=rstd[p][:, 1:2]).then_inc(qhi_made, 1)
            nc.scalar.activation(k_h1[p][0:DH, :], kd[p][0:DH, :], ACT.Copy).then_inc(kh1_made, 1)

        def values(i, b):
            act.wait_ge(vt_ready, i + 1)
            if not isinstance(i, int) or i >= 2:
                act.wait_ge(pv_done, 2 * i - 2)
            nc.scalar.activation(v_t[b][:, :, 0:3:2, :], ps_t[:, :, :].rearrange("p c (h d) -> p c h d", h=2),
                                 ACT.Copy).then_inc(v_made, 1)

        def max_row(i, p):
            act.wait_ge(row_ready, 2 * i + p + 1)
            nc.scalar.activation(q_lo[p][DH:DH + 1, :], ps_max[DH:DH + 1, 0, :], ACT.Copy).then_inc(row_made, 1)

        def exponents(i, p):
            if not isinstance(i, int) or i >= 1:
                act.wait_ge(pv_done, 2 * i + p - 1)
            for half in range(2):
                c = slice(half * KC // 2, (half + 1) * KC // 2)
                act.wait_ge(s_ready, 2 * (2 * i + p) + half + 1)
                act.sem_inc(act_passed, 1)
                nc.scalar.activation(probs[p][:, c, :], ps_s[:, c, :], ACT.Exp,
                                     scale=s_pair[:, bass.ts(i, 1)]).then_inc(exp_done, 1)

        def numerators(i, p):
            act.wait_ge(pv_done, 2 * i + p + 1)
            if not isinstance(i, int) or i >= 1:
                act.wait_ge(attn_made, i)
            rows = head_rows[p]
            nc.scalar.activation(numer[rows, :], ps_o[rows, :], ACT.Copy).then_inc(numer_made, 1)

        def tile_high(t):
            act.wait_ge(xt_ready, t + 1)
            nc.scalar.activation(xt[:, :, bass.ts(t, P)], ps_t[:, :, :], ACT.Copy).then_inc(xt_made, 1)

        def step(i, p, b):
            if within(i, p, -1):
                numerators(*((i - 1, 1) if p == 0 else (i, 0)))
            if within(i, p, 1):
                exponents(*((i, 1) if p == 0 else (i + 1, 0)))
            if p and (not isinstance(i, int) or i >= 2):
                tile_high(i - 2)
            if p == 0 and within(i, 0, 2):
                values(i + 1, 1 - b)
            if within(i, p, 3):
                highs(*((i + 1, 1) if p == 0 else (i + 2, 0)))
            if within(i, p, 2):
                max_row(i + 1, p)

        def weights_high(part):
            act.wait_ge(w_landed[part], part_sum(part))
            split_high(nc, weights, part, 0, whi_made)

        act.wait_ge(consts_made, 1)
        highs(0, 0)
        values(0, 0)
        max_row(0, 0)
        highs(0, 1)
        max_row(0, 1)
        act.wait_ge(scale_made, 1)
        exponents(0, 0)
        act.wait_ge(gate_turned, 1)
        nc.scalar.activation(gate_t[:, :, :], ps_t[:, :, 0:E], ACT.Copy).then_inc(gate_made, 1)
        highs(1, 0)
        for i in range(4):
            step(i, 0, i % 2)
            step(i, 1, i % 2)
        with act.Fori(0, (NT - 6) // 2) as k:
            for b in range(2):
                step(k * 2 + (4 + b), 0, b)
                step(k * 2 + (4 + b), 1, b)
        step(NT - 2, 0, 0)
        step(NT - 2, 1, 0)
        weights_high(0)
        step(NT - 1, 0, 1)
        weights_high(1)
        step(NT - 1, 1, 1)
        weights_high(2)
        numerators(NT - 1, 1)
        tile_high(NT - 2)
        for q in range(dims["early_logits"]):
            act.wait_ge(logits_ready, q + 1)
            nc.scalar.activation(logits_t[:, bass.ts(q, L)], ps_max[0:E, q % 2, :], ACT.Copy).then_inc(logits_made, 1)
        tile_high(NT - 1)

    @block.vector
    def _(dve):
        nc.vector.memset(zeros_f[:, :], 0.0).then_inc(consts_made, 1)
        nc.vector.memset(ones_f[:, :], 1.0)
        for b in range(2):
            last = nc.vector.memset(v_t[b][:, :, 1, :], 1.0)
        last.then_inc(consts_made, 1)
        dve.wait_ge(consts_made, 2)
        nc.vector.tensor_copy(ones_r[:, :], ones_f[:, :])
        for p in range(2):
            nc.vector.tensor_copy(q_lo[p][DH:96, :], zeros_f[DH:96, :])
            nc.vector.tensor_copy(k_h1[p][DH:96, :], zeros_f[DH:96, :]).then_inc(consts_made, 1)
        dve.wait_ge(consts_made, 4)
        for p in range(2):
            nc.vector.tensor_scalar(k_h1[p][DH:DH + 1, :], zeros_f[DH:DH + 1, :], 1.0, None,
                                    ALU.add).then_inc(consts_made, 1)
        dve.wait_ge(ident_made, 1)
        nc.vector.tensor_scalar(neg_ident[:, :], ident[:, :], -1.0, None, ALU.mult).then_inc(consts_made, 1)
        dve.wait_ge(len_landed, 16)
        nc.vector.tensor_copy(len_f[:, :], len_i[:, :]).then_inc(len_cast, 1)

        def head_stats(i, p):
            dve.wait_ge(x_landed[p], 32 * (i + 1))
            nc.vector.bn_stats(stats[p][:, :], xd[p][:, :]).then_inc(stats_raw, 1)
            if not isinstance(i, int) or i >= 1:
                dve.wait_ge(rstd_made, 2 * i + p - 1)
            dve.wait_ge(stats_raw, 2 * i + p + 1)
            dve.sem_inc(dve_passed, 1)
            nc.vector.bn_aggr(mv[p][:, :], stats[p][:, :]).then_inc(stats_made, 1)

        def key_low(i, p):
            dve.wait_ge(khi_made, 2 * i + p + 1)
            nc.vector.tensor_tensor(k_hl[p][DH:P, :], kd[p][DH:P, :], k_hl[p][DH:P, :].bitcast(F32),
                                    ALU.subtract).then_inc(klo_made, 1)

        def take_max(i, p, half):
            dve.wait_ge(max_ready, 2 * (2 * i + p) + half + 1)
            nc.vector.tensor_reduce(qmax[p][:, 2 * half:2 * half + 2], ps_max[:, :, :], AX.X,
                                    ALU.max).then_inc(max_taken, 1)

        def spread_max(i, p):
            dve.wait_ge(max_taken, 2 * (2 * i + p) + 2)
            if not isinstance(i, int) or i >= 1 or p:
                dve.wait_ge(row_ready, 2 * i + p)
            nc.vector.tensor_tensor(diag[:, :, :], neg_ident[:, :].unsqueeze(1).to_broadcast([P, KC, P]),
                                    qmax[p][:, :].unsqueeze(2).to_broadcast([P, KC, P]),
                                    ALU.mult).then_inc(diag_made, 1)

        def turn_sums(i, p):
            dve.wait_ge(pv_done, 2 * i + p + 1)
            if not isinstance(i, int) or i >= 1:
                dve.wait_ge(recip_made, 2 * i - 1)
            nc.vector.transpose(sums_t[head_rows[p], :], ps_o[head_rows[1 - p], :]).then_inc(sums_turned, 1)

        def normalize(i):
            dve.wait_ge(sums_turned, 2 * i + 2)
            nc.vector.reciprocal(recip_col[:, :],
                                 sums_t[:, :].rearrange("p (b c) -> p b c", c=32)[:, :, 0]).then_inc(recip_made, 1)
            dve.wait_ge(recip_made, 2 * i + 1)
            nc.vector.transpose(recip[:, :],
                                recip_col[:, :].unsqueeze(2).to_broadcast([P, L // 32, 32])).then_inc(recip_made, 1)
            dve.wait_ge(recip_made, 2 * i + 2)
            dve.wait_ge(numer_made, 2 * i + 2)
            if not isinstance(i, int) or i >= 1:
                dve.wait_ge(x1_made, i)
            nc.vector.tensor_tensor(attn[:, :], numer[:, :], recip[:, :], ALU.mult).then_inc(attn_made, 1)

        def tile_stats(t):
            dve.wait_ge(x1_made, t + 1)
            nc.vector.bn_stats(stats2[:, :], x1[:, t, :]).then_inc(stats2_raw, 1)
            dve.wait_ge(stats2_raw, t + 1)
            dve.sem_inc(dve_passed, 1)
            nc.vector.bn_aggr(mv2[:, :], stats2[:, :]).then_inc(stats2_made, 1)

        def tile_norm(t, b):
            dve.wait_ge(rstd2_made, t + 1)
            if not isinstance(t, int) or t >= 1:
                dve.wait_ge(xhat_stored, 16 * t)
            if not isinstance(t, int) or t >= 2:
                dve.wait_ge(xt_ready, t - 1)
            nc.vector.tensor_scalar(x_hat[b][:, :], x1[:, t, :], rstd2[:, 0:1], rstd2[:, 1:2], ALU.mult,
                                    ALU.add).then_inc(xhat_made, 1)

        for n in range(2):
            head_stats(0, n)
            key_low(0, n)
            if n == 0:
                dve.wait_ge(len_logged, 1)
                nc.vector.tensor_scalar(s_pair[:, :].rearrange("p (b h) -> p b h", b=B),
                                        len_ln[:, :].unsqueeze(2).to_broadcast([P, B, HEADS // 2]), SCALE, None,
                                        ALU.mult).then_inc(scale_made, 1)
            take_max(0, n, 0)
            take_max(0, n, 1)
            spread_max(0, n)
        head_stats(1, 0)
        key_low(1, 0)

        def step(i, p, b):
            if within(i, p, -1):
                turn_sums(*((i - 1, 1) if p == 0 else (i, 0)))
            if within(i, p, 2):
                take_max(i + 1, p, 0)
            if within(i, p, 3):
                head_stats(*((i + 1, 1) if p == 0 else (i + 2, 0)))
            if within(i, p, 2):
                take_max(i + 1, p, 1)
                spread_max(i + 1, p)
            if within(i, p, 3):
                key_low(*((i + 1, 1) if p == 0 else (i + 2, 0)))
            if p == 0 and within(i, p, -1):
                normalize(i - 1)
                if within(i, p, -4):
                    tile_norm(i - 2, b)
            if p and within(i, p, -2):
                tile_stats(i - 1)

        for i in range(4):
            step(i, 0, i % 2)
            step(i, 1, i % 2)
        with dve.Fori(0, (NT - 6) // 2) as k:
            for b in range(2):
                step(k * 2 + (4 + b), 0, b)
                step(k * 2 + (4 + b), 1, b)
        def weights_low(part):
            dve.wait_ge(whi_made, part + 1)
            split_low(nc, weights, part, 0, wlo_made)

        step(NT - 2, 0, 0)
        step(NT - 2, 1, 0)
        step(NT - 1, 0, 1)
        weights_low(0)
        step(NT - 1, 1, 1)
        tile_norm(NT - 2, 0)
        weights_low(1)
        turn_sums(NT - 1, 1)
        normalize(NT - 1)
        dve.wait_ge(whi_made, 4)
        weights_low(2)
        tile_stats(NT - 1)
        tile_norm(NT - 1, 1)

    @block.tensor
    def _(pe):
        def max_scores(i, p, half):
            pe.wait_ge(klo_made, 2 * i + p + 1)
            pe.wait_ge(qhi_made, 2 * i + p + 1)
            if half or p or not isinstance(i, int) or i >= 1:
                pe.wait_ge(max_taken, 2 * (2 * i + p) + half)
            if half == 0 and (p or not isinstance(i, int) or i >= 1):
                pe.wait_ge(row_made, 2 * i + p)
            for j in range(2):
                last = nc.tensor.matmul(ps_max[:, j, :], q_hi[p][:, bass.ts(2 * half + j, P)], k_hl[p][:, :],
                                        start=True, stop=True)
            last.then_inc(max_ready, 1)

        def turn_values(i, b, turns):
            pe.wait_ge(rows_landed[b], 16 * (turns + 1))
            if not isinstance(i, int) or i >= 1:
                pe.wait_ge(v_made, i)
            if not isinstance(i, int) or i >= 4:
                pe.wait_ge(xt_made, i - 3)
            for c in range(KC):
                last = nc.tensor.transpose(ps_t[:, c, :], k_rows[b][:, bass.ts(c, P)], ident[:, :])
            last.then_inc(vt_ready, 1)

        def spread_row(i, p):
            pe.wait_ge(diag_made, 2 * i + p + 1)
            nc.tensor.matmul(ps_max[:, 0, :], ones_r[:, :], diag[:, :, :], start=True,
                             stop=True).then_inc(row_ready, 1)

        def scores(i, p):
            if p or not isinstance(i, int) or i >= 1:
                pe.wait_ge(exp_done, 2 * (2 * i + p))
            for c in range(KC):
                nc.tensor.matmul(ps_s[:, c, :], k_hl[p][:, bass.ts(c, P)], q_hi[p][:, :], start=True, stop=False)
            pe.wait_ge(row_made, 2 * i + p + 1)
            pe.wait_ge(kh1_made, 2 * i + p + 1)
            pe.wait_ge(qlo_made, 2 * i + p + 1)
            for c in range(KC):
                last = nc.tensor.matmul(ps_s[:, c, :], k_h1[p][0:96, bass.ts(c, P)], q_lo[p][0:96, :],
                                        start=False, stop=True)
                if c % 2:
                    last.then_inc(s_ready, 1)

        def weigh_values(i, p, b, chunks):
            for c in chunks:
                if c == 0:
                    pe.wait_ge(v_made, i + 1)
                    if p or not isinstance(i, int) or i >= 1:
                        pe.wait_ge(numer_made, 2 * i + p)
                        pe.wait_ge(sums_turned, 2 * i + p)
                if c % 2 == 0:
                    pe.wait_ge(exp_done, 2 * (2 * i + p) + c // 2 + 1)
                last = nc.tensor.matmul(ps_o[:, :], v_t[b][:, c, p:p + 2, :], probs[p][:, c, :], start=c == 0,
                                        stop=c == KC - 1)
            if KC - 1 in chunks:
                last.then_inc(pv_done, 1)

        def turn_tile(t, b, values):
            pe.wait_ge(xhat_made, t + 1)
            pe.wait_ge(v_made, values)
            if not isinstance(t, int) or t >= 1:
                pe.wait_ge(xt_made, t)
            for c in range(KC):
                last = nc.tensor.transpose(ps_t[:, c, :], x_hat[b][:, bass.ts(c, P)], ident[:, :])
            last.then_inc(xt_ready, 1)

        def step(i, p, b, turns):
            if within(i, p, 1):
                scores(*((i, 1) if p == 0 else (i + 1, 0)))
            if within(i, p, 2):
                max_scores(i + 1, p, 0)
            if p and within(i, p, -4):
                turn_tile(i - 2, b, i + 2 if within(i, 0, 2) else NT)
            weigh_values(i, p, b, [0])
            if within(i, p, 2):
                max_scores(i + 1, p, 1)
            if p == 0 and within(i, p, 2):
                turn_values(i + 1, 1 - b, turns + b)
            weigh_values(i, p, b, [1, 2, 3])
            if within(i, p, 2):
                spread_row(i + 1, p)

        pe.wait_ge(ident_made, 1)
        pe.wait_ge(consts_made, 7)
        for n in range(2):
            max_scores(0, n, 0)
            if n == 0:
                turn_values(0, 0, 0)
            max_scores(0, n, 1)
            spread_row(0, n)
        scores(0, 0)
        pe.wait_ge(gate_landed, 16)
        pe.wait_ge(v_made, 1)
        for c in range(KC):
            last = nc.tensor.transpose(ps_t[:, c, 0:E], gate_sb[:, bass.ts(c, P)], ident[0:E, 0:E])
        last.then_inc(gate_turned, 1)
        pe.wait_ge(gate_made, 1)
        for i in range(4):
            step(i, 0, i % 2, i // 2)
            step(i, 1, i % 2, i // 2)
        with pe.Fori(0, (NT - 6) // 2) as k:
            for b in range(2):
                step(k * 2 + (4 + b), 0, b, k + 2)
                step(k * 2 + (4 + b), 1, b, k + 2)
        for i in range(NT - 2, NT):
            step(i, 0, i % 2, i // 2)
            step(i, 1, i % 2, i // 2)
        turn_tile(NT - 2, 0, NT)
        pe.wait_ge(row_made, NH)
        for q in range(dims["early_logits"]):
            pe.wait_ge(xt_made, (q + 1) * (L // P))
            for c in range(KC):
                last = nc.tensor.matmul(ps_max[0:E, q % 2, :], gate_t[:, c, :], xt[:, c, bass.ts(q, L)], start=c == 0,
                                        stop=c == KC - 1)
            last.then_inc(logits_ready, 1)
        turn_tile(NT - 1, 1, NT)


def experts_block(nc, ctx, dims, dram, keep):
    T, L, E, H = dims["T"], dims["L"], dims["E"], dims["H"]
    NT = T // P
    GROUP = 2 * P
    NS = T // GROUP
    NX = 2 * T // GROUP + E - 1
    KC = L // P
    MH = -(-H // P)
    HR = [min(P, H - m * P) for m in range(MH)]
    assert NS == 8 and NX % 2 == 1 and KC == 4 and MH == 3 and E == 8

    def sb(name, shape, dt=F32):
        return ctx.enter_context(nc.sbuf_tensor(name, shape, dt))

    def ps(name, shape, dt=F32):
        return ctx.enter_context(nc.psum_tensor(name, shape, dt))

    def sem(name):
        return ctx.enter_context(nc.semaphore(name))

    x1, xt, ident, ones_f = keep["x1"], keep["xt"], keep["ident"], keep["ones_f"]
    gate_t, logits_t, x_rows, weights = keep["gate_t"], keep["logits_t"], keep["x_rows"], keep["weights"]

    for half in ("hi", "lo"):
        weights[half].append([sb(f"w{n}_{half}1", [P, c, f], F32R)
                              for n, c, f in ((1, KC, H), (3, KC, H), (2, MH, L))])
    w_hi, w_lo = weights["hi"], weights["lo"]
    x_hi = [sb(f"x_hi{b}", [P, KC, GROUP], F32R) for b in range(2)]
    x_lo = [sb(f"x_lo{b}", [P, KC, GROUP], F32R) for b in range(2)]
    silu = sb("silu", [P, MH, GROUP])
    g_f = sb("g_f", [P, MH, GROUP])
    g_hi = sb("g_hi", [P, MH, GROUP], F32R)
    g_lo = sb("g_lo", [P, MH, GROUP], F32R)
    y_sb = [sb(f"y_sb{j}", [P, L]) for j in range(2)]
    slots_in = [sb(f"slots_in{p}", [P, 2, 2], U32) for p in range(2)]
    slots_out = [sb(f"slots_out{p}", [P, 2, 2], U32) for p in range(2)]

    e_neg = sb("e_neg", [P, NT, E])
    score = sb("score", [P, NT, E])
    top = sb("top", [P, NT, 8])
    top_i = sb("top_i", [P, NT, 8], U32)
    top_f = sb("top_f", [P, NT, 2])
    iota_e = sb("iota_e", [P, E])
    chosen = [sb(f"chosen{j}", [P, NT, E]) for j in range(2)]
    either = sb("either", [P, NT, E], BF16)
    top_sum = sb("top_sum", [P, NT])
    top_inv = sb("top_inv", [P, NT])
    upper = sb("upper", [P, P], BF16)
    ones_b = sb("ones_b", [P, P], BF16)
    running = sb("running", [P, E, NT])
    before = sb("before", [P, E])
    count = sb("count", [P, E])
    need = sb("need", [P, E])
    need_up = sb("need_up", [P, E])
    ends = sb("ends", [P, E])
    starts = sb("starts", [P, E])
    place_a = sb("place_a", [P, E, NT])
    picked = sb("picked", [P, NT, E])
    dest_f = sb("dest_f", [P, 2, NT])
    dest = sb("dest", [P, 2, NT], U32)
    entry = sb("entry", [P, NT, 2, 2], U32)
    iota_g = sb("iota_g", [1, NX + 1])
    past = sb("past", [1, NX + 1, E])
    group_f = sb("group_f", [1, NX + 1])
    group_e = sb("group_e", [1, NX + 1], I32)
    table = sb("table", [P, 2 * NX, 2], U32)

    ps_h = [ps(f"ps_h{m}", [P, 2, GROUP]) for m in range(MH)]
    ps_y = [ps(f"ps_y{j}", [P, L]) for j in range(2)]
    ps_x = [ps(f"ps_x{j}", [P, KC, P]) for j in range(2)]
    ps_r = ps("ps_r", [P, 4, P])

    names = """logits_ready logits_made logits_turned exp_made score_step
        top_made entry_iota iota_made either_made ranks_ready route_step dest_made group_made consts_set upper_zero
        upper_made table_preset table_filled table_landed xhi_made xlo_made hu_ready silu_made gf_made ghi_made
        glo_made y_ready y_taken out_stored upper_hi_made upper_lo_made lower_hi_made lower_lo_made ins_made outs_made
        turned add_done w1_landed w3_landed w2_landed entry_made gather_passed""".split()
    S = {n: sem(n) for n in names}
    x_landed = [sem(f"rows_landed{p}") for p in range(2)]
    w_landed = [S["w1_landed"], S["w3_landed"], S["w2_landed"]]

    out, xn, slot_table = dram["out"], dram["xn"], dram["slots"]
    block = ctx.enter_context(nc.Block("experts"))

    LAST = NS + NX - 1

    def at_least(v, bound):
        return not isinstance(v, int) or v >= bound

    def at_most(v, bound):
        return not isinstance(v, int) or v <= bound

    def run(eng, step, between=None):
        for G in range(2):
            step(G, G)
            if between is not None and G == 0:
                between()
        with eng.Fori(1, (NS - 2) // 2) as k:
            for b in range(2):
                step(k * 2 + b, b)
        for G in range(NS - 2, NS + 2):
            step(G, G % 2, G - NS, (G - NS) // 2)
        with eng.Fori(1, (NX - 3) // 2) as k:
            for b in range(2):
                step(k * 2 + (NS + b), b, k * 2 + b, k)
        for G in range(LAST - 2, LAST + 1):
            step(G, G % 2, G - NS, (G - NS) // 2)

    @block.sync
    def _(sp):
        def load(k, w, parts):
            for part in parts:
                if k is not None and at_least(k, 2):
                    if part < 2:
                        sp.wait_ge(S["upper_lo_made"], 2 * k - 3 + part)
                    else:
                        sp.wait_ge(S["lower_lo_made"], 2 * k - 2)
                load_part(sp, weights, part, w[part], w_landed[part])

        def load_group(s, parts):
            e = sp.value_load(group_e[0:1, bass.ds(s, 1)], min_val=0, max_val=E - 1)
            load(s + 1, [dram["w1"][e], dram["w3"][e], dram["w2"][e]], parts)

        def store(t):
            sp.wait_ge(S["y_taken"], t + 1)
            sp.dma_start(out[bass.ts(t, P), :], x1[:, t, :]).then_inc(S["out_stored"], 16)

        with sp.Fori(0, NS - 2) as t:
            store(t)
        sp.wait_ge(S["group_made"], 1)
        load_group(0, (0, 1, 2))
        for t in range(NS - 2, 2 * NS - 4):
            store(t)
        load_group(1, (0, 1))
        for t in range(2 * NS - 4, 2 * NS - 2):
            store(t)
        load_group(2, (0, 1))
        for t in range(2 * NS - 2, 2 * NS):
            store(t)
        load_group(1, (2,))
        with sp.Fori(3, NX) as s:
            load_group(s, (0, 1))
            load_group(s - 1, (2,))
        load_group(NX - 1, (2,))

    @block.gpsimd
    def _(pool):
        nc.gpsimd.memset(upper[:, :], 1.0).then_inc(S["upper_zero"], 1)
        pool.wait_ge(S["upper_zero"], 1)
        nc.gpsimd.affine_select(out=upper[:, :], in_=upper[:, :], compare_op=ALU.is_gt, fill=0.0, base=0,
                                pattern=[[1, P]], channel_multiplier=-1).then_inc(S["upper_made"], 1)
        nc.gpsimd.iota(iota_e[:, :], [[1, E]], base=0, channel_multiplier=0,
                       allow_small_or_imprecise_dtypes=True).then_inc(S["iota_made"], 1)
        nc.gpsimd.iota(iota_g[:, :], [[1, NX + 1]], base=0, channel_multiplier=0,
                       allow_small_or_imprecise_dtypes=True).then_inc(S["iota_made"], 1)
        nc.gpsimd.iota(entry[:, :, :, 0], [[P, NT], [0, 2]], base=0, channel_multiplier=1).then_inc(S["entry_iota"], 1)
        nc.gpsimd.iota(table[:, :, 0], [[0, 2 * NX]], base=T, channel_multiplier=1).then_inc(S["entry_iota"], 1)
        nc.gpsimd.iota(table[:, :, 1], [[0, 2 * NX]], base=0, channel_multiplier=0).then_inc(S["entry_iota"], 1)
        pool.wait_ge(S["entry_iota"], 3)
        table_dram = slot_table.rearrange("(g p) w -> p g w", p=P)
        pool.dma_start(table_dram, table[:, :, :]).then_inc(S["table_preset"], 16)
        pool.wait_ge(S["table_preset"], 16)
        pool.wait_ge(S["dest_made"], 1)
        pool.wait_ge(S["entry_made"], 1)
        for i in range(NT):
            for j in range(2):
                nc.gpsimd.indirect_dma_start(
                    slot_table, bass.IndirectOffsetOnAxis(ap=dest[:, j, i:i + 1], axis=0), entry[:, i, j, :],
                    None).then_inc(S["table_filled"], 16)
        pool.wait_ge(S["table_filled"], 16 * 2 * NT)
        pool.dma_start(table[:, :, :], table_dram).then_inc(S["table_landed"], 16)
        pool.wait_ge(S["table_landed"], 16)

        def slots_for(s, slots, made):
            if not isinstance(s, int):
                pool.sem_inc(S["gather_passed"], 1)
            nc.gpsimd.tensor_copy(slots[:, :, :], table[:, bass.ts(s, 2), :]).then_inc(made, 1)

        def fetch(s, p):
            if at_least(s, 2):
                pool.wait_ge(S["turned"], 2 * (s - 1))
            slots_for(s, slots_in[p], S["ins_made"])
            pool.wait_ge(S["ins_made"], s + 1)
            pool.sem_inc(S["gather_passed"], 1)
            for j in range(2):
                nc.gpsimd.indirect_dma_start(
                    x_rows[:, 2 * p + j, :], None, xn,
                    bass.IndirectOffsetOnAxis(ap=slots_in[p][:, j, 0:1], axis=0)).then_inc(x_landed[p], 16)

        def add(s, p):
            for j in range(2):
                pool.wait_ge(S["y_taken"], 2 * (NS + s) + j + 1)
                if j or at_least(s, 1):
                    pool.wait_ge(S["add_done"], 16 * (2 * s + j))
                pool.sem_inc(S["gather_passed"], 1)
                nc.gpsimd.indirect_dma_start(
                    out, bass.IndirectOffsetOnAxis(ap=slots_out[p][:, j, 0:1], axis=0), y_sb[j][:, :], None,
                    compute_op=ALU.add).then_inc(S["add_done"], 16)

        def step(s, p):
            add(s, p)
            if at_most(s, NX - 4):
                fetch(s + 3, 1 - p)
            if at_most(s, NX - 3):
                pool.wait_ge(S["add_done"], 32 * (s + 1))
                slots_for(s + 2, slots_out[p], S["outs_made"])

        for s in range(2):
            fetch(s, s)
            slots_for(s, slots_out[s], S["outs_made"])
        fetch(2, 0)
        pool.wait_ge(S["out_stored"], 16 * 2 * NS)
        for s in range(2):
            step(s, s)
        with pool.Fori(1, (NX - 3) // 2) as k:
            for p in range(2):
                step(k * 2 + p, p)
        for s in range(NX - 3, NX):
            step(s, s % 2)
        pool.wait_ge(S["add_done"], 32 * NX)

    @block.scalar
    def _(act):
        def split_x(G, b, j, s=None):
            if at_least(G, 2):
                act.wait_ge(S["hu_ready"], 3 * (G - 1))
            if s is None:
                source = xt[:, :, bass.ds(G * GROUP + j * P, P)]
            else:
                act.wait_ge(S["turned"], 2 * s + j + 1)
                source = ps_x[j][:, :, :]
            nc.scalar.activation(x_hi[b][:, :, bass.ts(j, P)], source, ACT.Copy).then_inc(S["xhi_made"], 1)

        def gate(G, m):
            act.wait_ge(S["hu_ready"], 3 * G + m + 1)
            if at_least(G, 1):
                act.wait_ge(S["gf_made"], 3 * G + m - 2)
            nc.scalar.activation(silu[0:HR[m], m, :], ps_h[m][0:HR[m], 0, :], ACT.Silu).then_inc(S["silu_made"], 1)

        def weight_y(G, s, p):
            for j in range(2):
                act.wait_ge(S["y_ready"], 2 * G + j + 1)
                act.wait_ge(S["outs_made"], s + 1)
                if at_least(s, 1):
                    act.wait_ge(S["add_done"], 16 * (2 * s - 1 + j))
                nc.scalar.activation(y_sb[j][:, :], ps_y[j][:, :], ACT.Copy,
                                     scale=slots_out[p][:, j, 1:2].bitcast(F32)).then_inc(S["y_taken"], 1)

        def upper_high(k, p, part):
            act.wait_ge(S["hu_ready"], 3 * (k + (NS - 2)))
            act.wait_ge(w_landed[part], 16 * k)
            split_high(nc, weights, part, p, S["upper_hi_made"])

        def lower_high(k, p):
            act.wait_ge(S["y_ready"], 2 * (k + (NS - 2)))
            act.wait_ge(w_landed[2], 32 * k)
            split_high(nc, weights, 2, p, S["lower_hi_made"])

        for G in range(2):
            for j in range(2):
                split_x(G, G, j)
        for n, q in enumerate(range(dims["early_logits"], T // L)):
            act.wait_ge(S["logits_ready"], n + 1)
            nc.scalar.activation(logits_t[:, bass.ts(q, L)], ps_y[n % 2][0:E, :], ACT.Copy).then_inc(S["logits_made"], 1)
        act.wait_ge(S["logits_turned"], 1)
        nc.scalar.activation(e_neg[:, :, :], ps_r[:, 0, :].rearrange("p (i e) -> p i e", e=E), ACT.Exp,
                             scale=-1.0).then_inc(S["exp_made"], 1)
        for m in range(MH):
            gate(0, m)

        def step(G, b, s=None, h=None):
            routed_2 = s is not None and at_least(s, -2) and at_most(s, NX - 3)
            if routed_2:
                upper_high(s + 3, 1 - b, 0)
                upper_high(s + 3, 1 - b, 1)
            if at_most(G, LAST - 1):
                gate(G + 1, 0)
            if s is not None and at_least(s, 0):
                weight_y(G, s, b)
            if s is None:
                for j in range(2):
                    split_x(G + 2, b, j)
            elif routed_2:
                for j in range(2):
                    split_x(G + 2, b, j, s + 2)
            if s is not None and at_least(s, -1) and at_most(s, NX - 2):
                lower_high(s + 2, b)
            if at_most(G, LAST - 1):
                gate(G + 1, 1)
                gate(G + 1, 2)

        run(act, step)

    @block.vector
    def _(dve):
        def split_x(G, b, j, s=None):
            dve.wait_ge(S["xhi_made"], 2 * G + j + 1)
            source = xt[:, :, bass.ds(G * GROUP + j * P, P)] if s is None else ps_x[j][:, :, :]
            nc.vector.tensor_tensor(x_lo[b][:, :, bass.ts(j, P)], source, x_hi[b][:, :, bass.ts(j, P)].bitcast(F32),
                                    ALU.subtract).then_inc(S["xlo_made"], 1)

        def hidden(G, m):
            r = HR[m]
            dve.wait_ge(S["silu_made"], 3 * G + m + 1)
            nc.vector.tensor_tensor(g_f[0:r, m, :], silu[0:r, m, :], ps_h[m][0:r, 1, :],
                                    ALU.mult).then_inc(S["gf_made"], 1)
            dve.wait_ge(S["gf_made"], 3 * G + m + 1)
            if at_least(G, 1):
                dve.wait_ge(S["y_ready"], 2 * G)
            nc.vector.tensor_copy(g_hi[0:r, m, :], g_f[0:r, m, :]).then_inc(S["ghi_made"], 1)
            dve.wait_ge(S["ghi_made"], 3 * G + m + 1)
            nc.vector.tensor_tensor(g_lo[0:r, m, :], g_f[0:r, m, :], g_hi[0:r, m, :].bitcast(F32),
                                    ALU.subtract).then_inc(S["glo_made"], 1)

        def add_x1(G):
            for j in range(2):
                dve.wait_ge(S["y_ready"], 2 * G + j + 1)
                t = G * 2 + j
                nc.vector.tensor_tensor(x1[:, t, :], ps_y[j][:, :], x1[:, t, :], ALU.add).then_inc(S["y_taken"], 1)

        def upper_low(k, p, part):
            dve.wait_ge(S["upper_hi_made"], 2 * k - 1 + part)
            split_low(nc, weights, part, p, S["upper_lo_made"])

        def lower_low(k, p):
            dve.wait_ge(S["lower_hi_made"], 2 * k)
            split_low(nc, weights, 2, p, S["lower_lo_made"])

        def scores():
            dve.wait_ge(S["exp_made"], 1)
            nc.vector.tensor_scalar(e_neg[:, :, :], e_neg[:, :, :], 1.0, None, ALU.add).then_inc(S["score_step"], 1)
            dve.wait_ge(S["score_step"], 1)
            nc.vector.reciprocal(score[:, :, :], e_neg[:, :, :]).then_inc(S["score_step"], 1)
            dve.wait_ge(S["score_step"], 2)
            for i in range(NT):
                nc.vector.max(top[:, i, :], score[:, i, :]).then_inc(S["top_made"], 1)
            for i in range(NT):
                dve.wait_ge(S["top_made"], i + 1)
                last = nc.vector.max_index(top_i[:, i, :], top[:, i, :], score[:, i, :])
            last.then_inc(S["score_step"], 1)
            dve.wait_ge(S["score_step"], 3)
            nc.vector.tensor_copy(top_f[:, :, :], top_i[:, :, 0:2]).then_inc(S["score_step"], 1)
            dve.wait_ge(S["score_step"], 4)
            dve.wait_ge(S["iota_made"], 2)
            for j in range(2):
                nc.vector.tensor_tensor(chosen[j][:, :, :], iota_e[:, :].unsqueeze(1).to_broadcast([P, NT, E]),
                                        top_f[:, :, j:j + 1].to_broadcast([P, NT, E]),
                                        ALU.is_equal).then_inc(S["score_step"], 1)
            dve.wait_ge(S["score_step"], 6)
            nc.vector.tensor_tensor(either[:, :, :], chosen[0][:, :, :], chosen[1][:, :, :],
                                    ALU.add).then_inc(S["either_made"], 1)
            nc.vector.tensor_tensor(top_sum[:, :], top[:, :, 0], top[:, :, 1], ALU.add).then_inc(S["score_step"], 1)
            dve.wait_ge(S["score_step"], 7)
            nc.vector.tensor_scalar(top_sum[:, :], top_sum[:, :], 1e-20, None, ALU.add).then_inc(S["score_step"], 1)
            dve.wait_ge(S["score_step"], 8)
            nc.vector.reciprocal(top_inv[:, :], top_sum[:, :]).then_inc(S["score_step"], 1)
            dve.wait_ge(S["score_step"], 9)
            for j in range(2):
                nc.vector.scalar_tensor_tensor(entry[:, :, j, 1].bitcast(F32), top[:, :, j], dims["routed_scale"],
                                               top_inv[:, :], ALU.mult, ALU.mult).then_inc(S["score_step"], 1)
            dve.wait_ge(S["score_step"], 11)
            dve.wait_ge(S["entry_iota"], 3)
            dve.sem_inc(S["entry_made"], 1)


        def places():
            ranks = ps_r[:, 1, :].rearrange("p (e i) -> p e i", e=E)
            totals = ps_r[:, 2, :]
            steps = [0]

            def routed(ins):
                steps[0] += 1
                ins.then_inc(S["route_step"], 1)
                dve.wait_ge(S["route_step"], steps[0])

            dve.wait_ge(S["ranks_ready"], 1)
            routed(nc.vector.tensor_tensor_scan(running[:, :, :].rearrange("p e i -> p (e i)"), ones_f[:, 0:E * NT], totals,
                                                0.0, ALU.mult, ALU.add))
            routed(nc.vector.memset(before[:, 0:1], 0.0))
            routed(nc.vector.tensor_copy(before[:, 1:E], running[:, 0:E - 1, NT - 1]))
            routed(nc.vector.tensor_tensor(count[:, :], running[:, :, NT - 1], before[:, :], ALU.subtract))
            routed(nc.vector.tensor_scalar(need[:, :], count[:, :], 1.0 / GROUP, 0.5 - 0.5 / GROUP, ALU.mult, ALU.add))
            routed(nc.vector.tensor_scalar(need_up[:, :], need[:, :], 8388608.0, None, ALU.add))
            routed(nc.vector.tensor_scalar(need[:, :], need_up[:, :], -8388608.0, None, ALU.add))
            routed(nc.vector.tensor_tensor_scan(ends[:, :], ones_f[:, 0:E], need[:, :], 0.0, ALU.mult, ALU.add))
            routed(nc.vector.tensor_tensor(past[:, :, :], ends[0:1, :].unsqueeze(1).to_broadcast([1, NX + 1, E]),
                                           iota_g[:, :].unsqueeze(2).to_broadcast([1, NX + 1, E]), ALU.is_le))
            routed(nc.vector.tensor_reduce(group_f[:, :], past[:, :, :], AX.X, ALU.add))
            nc.vector.tensor_scalar(group_e[:, :], group_f[:, :], float(E - 1), None, ALU.min).then_inc(S["group_made"], 1)
            routed(nc.vector.tensor_tensor(starts[:, :], ends[:, :], need[:, :], ALU.subtract))
            routed(nc.vector.scalar_tensor_tensor(starts[:, :], starts[:, :], float(GROUP), before[:, :], ALU.mult,
                                                  ALU.subtract))
            routed(nc.vector.tensor_tensor(place_a[:, :, :].rearrange("p e i -> p (e i)"),
                                           running[:, :, :].rearrange("p e i -> p (e i)"), totals, ALU.subtract))
            routed(nc.vector.tensor_tensor(place_a[:, :, :], place_a[:, :, :], ranks, ALU.add))
            routed(nc.vector.tensor_tensor(place_a[:, :, :], place_a[:, :, :],
                                           starts[:, :].unsqueeze(2).to_broadcast([P, E, NT]), ALU.add))
            for j in range(2):
                routed(nc.vector.tensor_tensor(picked[:, :, :], chosen[j][:, :, :],
                                               place_a[:, :, :].rearrange("p e i -> p i e"), ALU.mult))
                routed(nc.vector.tensor_reduce(dest_f[:, j, :], picked[:, :, :], AX.X, ALU.add))
            nc.vector.tensor_copy(dest[:, :, :], dest_f[:, :, :]).then_inc(S["dest_made"], 1)


        def step(G, b, s=None, h=None):
            routed_2 = s is not None and at_least(s, -2) and at_most(s, NX - 3)
            if routed_2:
                upper_low(s + 3, 1 - b, 0)
                upper_low(s + 3, 1 - b, 1)
            if s is None or not at_least(s, 0):
                add_x1(G)
            if at_most(G, LAST - 1):
                hidden(G + 1, 0)
            if s is None:
                for j in range(2):
                    split_x(G + 2, b, j)
            elif routed_2:
                for j in range(2):
                    split_x(G + 2, b, j, s + 2)
            if s is not None and at_least(s, -1) and at_most(s, NX - 2):
                lower_low(s + 2, b)
            if at_most(G, LAST - 1):
                hidden(G + 1, 1)
                hidden(G + 1, 2)

        nc.vector.memset(ones_b[:, :], 1.0).then_inc(S["consts_set"], 1)
        for G in range(2):
            for j in range(2):
                split_x(G, G, j)
        scores()
        for m in range(MH):
            hidden(0, m)
        run(dve, step, places)

    @block.tensor
    def _(pe):
        def up(G, b, tiles, k, p):
            pe.wait_ge(S["xlo_made"], 2 * G + 2)
            if k is not None:
                pe.wait_ge(S["upper_lo_made"], 2 * k)
            for m in tiles:
                cols = slice(m * P, m * P + HR[m])
                if at_least(G, 1):
                    pe.wait_ge(S["gf_made"], 3 * G + m - 2)
                for part in range(2):
                    acc = ps_h[m][0:HR[m], part, :]
                    hi, lo = w_hi[p][part], w_lo[p][part]
                    for c in range(KC):
                        nc.tensor.matmul(acc, hi[:, c, cols], x_hi[b][:, c, :], start=c == 0, stop=False)
                        nc.tensor.matmul(acc, hi[:, c, cols], x_lo[b][:, c, :], start=False, stop=False)
                        last = nc.tensor.matmul(acc, lo[:, c, cols], x_hi[b][:, c, :], start=False, stop=c == KC - 1)
                last.then_inc(S["hu_ready"], 1)

        def down(G, k, p):
            if k is not None:
                pe.wait_ge(S["lower_lo_made"], 2 * k)
            hi, lo = w_hi[p][2], w_lo[p][2]
            for j in range(2):
                if at_least(G, 1):
                    pe.wait_ge(S["y_taken"], 2 * G + j - 1)
                for m in range(MH):
                    pe.wait_ge(S["glo_made"], 3 * G + m + 1)
                    r, tokens = HR[m], bass.ts(j, P)
                    nc.tensor.matmul(ps_y[j][:, :], g_hi[0:r, m, tokens], hi[0:r, m, :], start=m == 0, stop=False)
                    nc.tensor.matmul(ps_y[j][:, :], g_hi[0:r, m, tokens], lo[0:r, m, :], start=False, stop=False)
                    last = nc.tensor.matmul(ps_y[j][:, :], g_lo[0:r, m, tokens], hi[0:r, m, :], start=False,
                                            stop=m == MH - 1)
                last.then_inc(S["y_ready"], 1)

        def turn(s, h, p):
            pe.wait_ge(x_landed[p], 32 * (h + 1))
            for j in range(2):
                if at_least(s, 1):
                    pe.wait_ge(S["xlo_made"], 2 * (s + NS) + j - 1)
                for c in range(KC):
                    last = nc.tensor.transpose(ps_x[j][:, c, :], x_rows[:, 2 * p + j, bass.ts(c, P)], ident[:, :])
                last.then_inc(S["turned"], 1)

        late = T // L - dims["early_logits"]
        for n, q in enumerate(range(dims["early_logits"], T // L)):
            for c in range(KC):
                last = nc.tensor.matmul(ps_y[n % 2][0:E, :], gate_t[:, c, :], xt[:, c, bass.ts(q, L)], start=c == 0,
                                        stop=c == KC - 1)
            last.then_inc(S["logits_ready"], 1)
        pe.wait_ge(S["logits_made"], late)
        for i in range(NT):
            last = nc.tensor.transpose(ps_r[:, 0, i * E:(i + 1) * E], logits_t[:, bass.ts(i, P)], ident[0:E, 0:E])
        last.then_inc(S["logits_turned"], 1)
        up(0, 0, range(MH), None, 0)

        def count_ranks():
            pe.wait_ge(S["either_made"], 1)
            pe.wait_ge(S["upper_made"], 1)
            pe.wait_ge(S["consts_set"], 1)
            by_expert = either[:, :, :].rearrange("p i e -> p e i")
            nc.tensor.matmul(ps_r[:, 1, :], upper[:, :], by_expert, start=True, stop=True)
            nc.tensor.matmul(ps_r[:, 2, :], ones_b[:, :], by_expert, start=True, stop=True).then_inc(S["ranks_ready"], 1)

        def step(G, b, s=None, h=None):
            routed, routed_1 = s is not None and at_least(s, 0), s is not None and at_least(s, -1)
            set_1 = (s + 2, b) if routed_1 else (None, 0)
            if at_most(G, LAST - 1):
                up(G + 1, 1 - b, [0], *set_1)
            if isinstance(G, int) and G == 0:
                count_ranks()
            down(G, *((s + 1, 1 - b) if routed else (None, 0)))
            if s is not None and at_least(s, -2) and at_most(s, NX - 3):
                turn(s + 2, h + 1, b)
            if at_most(G, LAST - 1):
                up(G + 1, 1 - b, [1, 2], *set_1)

        run(pe, step)


def build(nc, ins, out):
    x = ins["x"]
    B, C, L = x.shape
    E, _, H = ins["L0_ffn_w1"].shape
    T = B * C
    NT = T // P
    NX = 2 * T // (2 * P) + E - 1
    dims = {"B": B, "C": C, "L": L, "T": T, "E": E, "H": H, "routed_scale": 2.5, "early_logits": 2}
    dram = {
        "x": x, "ctx": ins["ctx_2048"], "lengths": ins["itok_B_779_1933"], "out": out,
        "gate": ins["L0_ffn_gate_w"], "w1": ins["L0_ffn_w1"], "w2": ins["L0_ffn_w2"], "w3": ins["L0_ffn_w3"],
        "sw1": ins["L0_ffn_sw1"], "sw2": ins["L0_ffn_sw2"], "sw3": ins["L0_ffn_sw3"],
        "xn": nc.dram_tensor("xn", (T + P, L), F32, kind="Internal").ap(),
        "slots": nc.dram_tensor("slots", (NX * 2 * P, 2), U32, kind="Internal").ap(),
    }
    with ExitStack() as common:
        def sb(name, shape, dt=F32):
            return common.enter_context(nc.sbuf_tensor(name, shape, dt))

        keep = {"x1": sb("x1", [P, NT, L]), "xt": sb("xt", [P, L // P, T]), "ident": sb("ident", [P, P]),
                "ones_f": sb("ones_f", [P, P]), "gate_t": sb("gate_t", [P, L // P, E])}
        rows = sb("x_rows", [P, 4, L])
        keep["x_rows"] = rows
        keep["logits_t"] = rows[0:E, :, :].rearrange("e q l -> e (q l)")
        KC, MH = L // P, -(-H // P)
        shapes = ((1, KC, H), (3, KC, H), (2, MH, L))
        keep["weights"] = {"f": [sb(f"w{n}_f", [P, c, f]) for n, c, f in shapes], "last_rows": H - (MH - 1) * P}
        for half in ("hi", "lo"):
            keep["weights"][half] = [[sb(f"w{n}_{half}0", [P, c, f], F32R) for n, c, f in shapes]]
        for stage in (attention_block, experts_block):
            with ExitStack() as ctx:
                stage(nc, ctx, dims, dram, keep)


_INS = ['x', 'ctx_2048', 'itok_B_779_1933', 'L0_ffn_gate_w', 'L0_ffn_w1', 'L0_ffn_w2', 'L0_ffn_w3', 'L0_ffn_sw1',
        'L0_ffn_sw2', 'L0_ffn_sw3']


def kernel(**inputs):
    import concourse.bacc as _bacc
    from concourse.bass_utils import run_bass_kernel_spmd as _run

    nc = _bacc.Bacc("TRN2", target_bir_lowering=False, num_devices=1)
    arrays, aps = {}, {}
    for name in _INS:
        a = np.ascontiguousarray(inputs[name])
        arrays[f"in_{name}_dram"] = a
        aps[name] = nc.dram_tensor(f"in_{name}_dram", a.shape, mybir.dt.from_np(a.dtype), kind="ExternalInput").ap()
    shape = inputs["x"].shape
    rows = shape[0] * shape[1]
    out = nc.dram_tensor("out_0_dram", (rows + P, shape[2]), F32, kind="ExternalOutput").ap()
    build(nc, aps, out)
    r = _run(nc, [arrays], core_ids=[0])
    return r.results[0]["out_0_dram"][:rows].reshape(shape)
```

```python
from contextlib import ExitStack

import numpy as np

import concourse.bass as bass
from concourse import mybir

ALU = mybir.AluOpType
ACT = mybir.ActivationFunctionType
AX = mybir.AxisListType
F32 = mybir.dt.float32
F32R = mybir.dt.float32r
BF16 = mybir.dt.bfloat16
I32 = mybir.dt.int32
U32 = mybir.dt.uint32

P = 128
EPS = 1e-5
HEADS = 8
DH = 64
SCALE = 1.0 / (DH ** 0.5 * float(np.log(20)))


def spread_blocks(sp, blocks, rows, landed):
    for a in range(4):
        sp.dma_start(blocks[a * 32:(a + 1) * 32], rows[:, bass.ts(a, P)]).then_inc(landed, 16)


def turn_blocks(nc, turned, blocks):
    return nc.vector.transpose(turned.rearrange("p c (i q) -> p q c i", q=4),
                               blocks.rearrange("p q (i c) -> p q c i", c=turned.shape[1]))


def part_sum(part):
    return 32 if part == 2 else 16


def load_part(sp, weights, part, w, landed):
    f = weights["f"][part]
    if part < 2:
        sp.dma_start(f[:, :, :], w.rearrange("(p c) h -> p c h", p=P)).then_inc(landed, 16)
        return
    m = f.shape[1] - 1
    H = w.shape[0]
    sp.dma_start(f[:, 0:m, :], w[0:m * P].rearrange("(m p) n -> p m n", p=P)).then_inc(landed, 16)
    sp.dma_start(f[0:H - m * P, m, :], w[m * P:H]).then_inc(landed, 16)


def split_high(nc, weights, part, p, made):
    f, hi = weights["f"][part], weights["hi"][p][part]
    if part < 2:
        nc.scalar.activation(hi[:, :, :], f[:, :, :], ACT.Copy).then_inc(made, 1)
        return
    m, r = f.shape[1] - 1, weights["last_rows"]
    nc.scalar.activation(hi[:, 0:m, :], f[:, 0:m, :], ACT.Copy).then_inc(made, 1)
    nc.scalar.activation(hi[0:r, m, :], f[0:r, m, :], ACT.Copy).then_inc(made, 1)


def split_low(nc, weights, part, p, made):
    f, hi, lo = weights["f"][part], weights["hi"][p][part], weights["lo"][p][part]
    if part < 2:
        nc.vector.tensor_tensor(lo[:, :, :], f[:, :, :], hi[:, :, :].bitcast(F32), ALU.subtract).then_inc(made, 1)
        return
    m, r = f.shape[1] - 1, weights["last_rows"]
    nc.vector.tensor_tensor(lo[:, 0:m, :], f[:, 0:m, :], hi[:, 0:m, :].bitcast(F32), ALU.subtract).then_inc(made, 1)
    nc.vector.tensor_tensor(lo[0:r, m, :], f[0:r, m, :], hi[0:r, m, :].bitcast(F32), ALU.subtract).then_inc(made, 1)


def attention_block(nc, ctx, dims, dram, keep):
    B, C, L = dims["B"], dims["C"], dims["L"]
    NH = B * HEADS
    NT = B * C // P
    KC = L // P

    def sb(name, shape, dt=F32):
        return ctx.enter_context(nc.sbuf_tensor(name, shape, dt))

    def sem(name):
        return ctx.enter_context(nc.semaphore(name))

    x1, xt = keep["x1"], keep["xt"]
    ident, ones_f = keep["ident"], keep["ones_f"]
    gate_t, logits_t, weights = keep["gate_t"], keep["logits_t"], keep["weights"]
    E, H = dims["E"], dims["H"]

    xd = [sb(f"xd{p}", [P, L]) for p in range(2)]
    kd = [sb(f"kd{p}", [P, L]) for p in range(2)]
    k_rows = [sb(f"k_rows{p}", [P, 4, P]) for p in range(2)]
    q_f = sb("q_f", [DH, L])
    q_hi = [sb(f"q_hi{p}", [P, L], F32R) for p in range(2)]
    q_lo = [sb(f"q_lo{p}", [P, L], F32R) for p in range(2)]
    k_hl = [sb(f"k_hl{p}", [P, L], F32R) for p in range(2)]
    k_h1 = [sb(f"k_h1{p}", [P, L], F32R) for p in range(2)]
    v_t = [sb(f"v_t{p}", [P, KC, 3, DH]) for p in range(2)]
    probs = [sb(f"probs{p}", [P, KC, L]) for p in range(2)]
    diag = sb("diag", [P, KC, P], F32R)
    numer = sb("numer", [P, L])
    sums_t = sb("sums_t", [P, L])
    recip_col = sb("recip_col", [P, L // 32])
    recip = sb("recip", [P, L])
    attn = sb("attn", [P, L])
    x_hat = [sb(f"x_hat{p}", [P, L]) for p in range(3)]
    x_blocks = [sb(f"x_blocks{p}", [P, 4, P]) for p in range(2)]
    x_turned = sb("x_turned", [P, KC, P])
    gate_sb = sb("gate_sb", [E, L])
    neg_ident = sb("neg_ident", [P, P])
    ones_r = sb("ones_r", [P, P], F32R)
    zeros_f = sb("zeros_f", [P, L])
    stats = [sb(f"stats{p}", [P, 6]) for p in range(2)]
    mv = [sb(f"mv{p}", [P, 2]) for p in range(2)]
    rstd = [sb(f"rstd{p}", [P, 2]) for p in range(2)]
    var_e = sb("var_e", [P, 1])
    minus_half = sb("minus_half", [P, 1])
    stats2 = sb("stats2", [P, 6])
    mv2 = sb("mv2", [P, 2])
    rstd2 = sb("rstd2", [P, 2])
    qmax = [sb(f"qmax{p}", [P, KC]) for p in range(2)]
    len_i = sb("len_i", [P, B], I32)
    len_f = sb("len_f", [P, B])
    len_ln = sb("len_ln", [P, B])
    s_pair = sb("s_pair", [P, NH // 2])

    ps_max = ctx.enter_context(nc.psum_tensor("ps_max", [P, 2, L], F32))
    ps_s = ctx.enter_context(nc.psum_tensor("ps_s", [P, KC, L], F32))
    ps_o = [ctx.enter_context(nc.psum_tensor(f"ps_o{p}", [P, L], F32)) for p in range(2)]

    len_landed = sem("len_landed")
    x1_landed = sem("x1_landed")
    x_landed = [sem(f"x_landed{p}") for p in range(2)]
    k_landed = [sem(f"k_landed{p}") for p in range(2)]
    rows_landed = [sem(f"k_rows_landed{p}") for p in range(2)]
    pad_stored = sem("pad_stored")
    ident_zero = sem("ident_zero")
    ident_made = sem("ident_made")
    consts_made = sem("consts_made")
    len_cast = sem("len_cast")
    len_logged = sem("len_logged")
    scale_made = sem("scale_made")
    stats_raw = sem("stats_raw")
    stats_made = sem("stats_made")
    rstd_step = sem("rstd_step")
    rstd_made = sem("rstd_made")
    qhi_made = sem("qhi_made")
    khi_made = sem("khi_made")
    kh1_made = sem("kh1_made")
    qf_made = sem("qf_made")
    qlo_made = sem("qlo_made")
    klo_made = sem("klo_made")
    max_ready = sem("max_ready")
    max_taken = sem("max_taken")
    diag_made = sem("diag_made")
    row_ready = sem("row_ready")
    row_made = sem("row_made")
    v_made = sem("v_made")
    s_ready = sem("s_ready")
    exp_done = sem("exp_done")
    pv_done = sem("pv_done")
    numer_made = sem("numer_made")
    sums_turned = sem("sums_turned")
    recip_made = sem("recip_made")
    attn_made = sem("attn_made")
    x1_made = sem("x1_made")
    stats2_raw = sem("stats2_raw")
    stats2_made = sem("stats2_made")
    rstd2_made = sem("rstd2_made")
    xhat_made = sem("xhat_made")
    xhat_stored = sem("xhat_stored")
    blocks_landed = sem("blocks_landed")
    last_landed = sem("last_landed")
    blocks_turned = sem("blocks_turned")
    xt_made = sem("xt_made")
    gate_landed = sem("gate_landed")
    gate_turned = sem("gate_turned")
    gate_made = sem("gate_made")
    logits_ready = sem("logits_ready")
    logits_made = sem("logits_made")
    w_landed = [sem(f"shared_w{n}_landed") for n in (1, 3, 2)]
    whi_made = sem("shared_whi_made")
    wlo_made = sem("shared_wlo_made")
    pool_passed, act_passed, dve_passed, sp_passed = (sem(f"{e}_passed") for e in ("pool", "act", "dve", "sp"))

    x_rows = dram["x"].rearrange("b (h d) l -> (b h) d l", d=DH)
    c_rows = dram["ctx"].rearrange("b (h d) l -> (b h) d l", d=DH)
    xn_rows = dram["xn"]
    k_pairs = dram["ctx"].rearrange("b (i g j) (a f) -> (b i) a j g f", g=4, j=32, a=4)
    head_rows = [slice(0, DH), slice(DH, P)]

    def within(i, p, ahead=0):
        return not isinstance(i, int) or 0 <= 2 * i + p + ahead < NH

    block = ctx.enter_context(nc.Block("attention"))

    @block.sync
    def _(sp):
        def load(i, b):
            for p in range(2):
                if not isinstance(i, int) or i >= 1:
                    heads = 2 * i + (p - 1)
                    if not isinstance(i, int):
                        heads = sp.snap(heads)
                    sp.wait_ge(klo_made, heads)
                    sp.wait_ge(qlo_made, heads)
                    sp.wait_ge(kh1_made, heads)
                    sp.sem_inc(sp_passed, 1)
                for half in head_rows:
                    sp.dma_start(xd[p][half, :], x_rows[2 * i + p]).then_inc(x_landed[p], 16)
                for half in head_rows:
                    sp.dma_start(kd[p][half, :], c_rows[2 * i + p]).then_inc(k_landed[p], 16)
            if not isinstance(i, int) or i >= 2:
                pairs = i - 1 if isinstance(i, int) else sp.snap(i - 1)
                sp.wait_ge(v_made, pairs)
                sp.sem_inc(sp_passed, 1)
            for a in range(4):
                sp.dma_start(k_rows[b][a * 32:(a + 1) * 32, :, :], k_pairs[i, a]).then_inc(rows_landed[b], 16)

        def store(t, b, rows):
            made, turned = t + 1, t - 1
            if not isinstance(t, int):
                made, turned = sp.snap(made), sp.snap(turned)
            sp.wait_ge(xhat_made, made)
            if not isinstance(t, int):
                sp.sem_inc(sp_passed, 1)
            if not isinstance(t, int) or t >= 2:
                sp.wait_ge(blocks_turned, turned)
            if not isinstance(t, int):
                sp.sem_inc(sp_passed, 1)
            spread_blocks(sp, x_blocks[b], x_hat[rows], blocks_landed if rows < 2 else last_landed)
            sp.dma_start(xn_rows[bass.ts(t, P), :], x_hat[rows][:, :]).then_inc(xhat_stored, 16)

        def load_x1(tiles):
            rows = dram["x"].rearrange("b (t p) l -> p (b t) l", p=P)
            sp.dma_start(x1[:, tiles, :], rows[:, tiles]).then_inc(x1_landed, 16)

        load(0, 0)
        sp.dma_start(len_i[:, :], dram["lengths"].partition_broadcast(P)).then_inc(len_landed, 16)
        sp.dma_start(gate_sb[:, :], dram["gate"]).then_inc(gate_landed, 16)
        load_x1(slice(0, NT // 2))
        load(1, 1)
        sp.wait_ge(consts_made, 1)
        sp.dma_start(xn_rows[NT * P:NT * P + P, :], zeros_f[:, :]).then_inc(pad_stored, 16)
        sp.dma_start(dram["out"][NT * P:NT * P + P, :], zeros_f[:, :]).then_inc(pad_stored, 16)
        load(2, 0)
        load_x1(slice(NT // 2, NT))
        load(3, 1)
        for i in range(4, 6):
            load(i, i % 2)
            store(i - 4, i % 2, i % 2)
        with sp.Fori(1, (NT - 4) // 2) as k:
            for b in range(2):
                load(k * 2 + (4 + b), b)
                store(k * 2 + b, b, b)
        for n, w in enumerate((dram["sw1"], dram["sw3"], dram["sw2"])):
            load_part(sp, weights, n, w, w_landed[n])
        for t in range(NT - 4, NT):
            store(t, t % 2, 2 if t == NT - 1 else t % 2)
        sp.wait_ge(xhat_stored, 16 * NT)
        sp.wait_ge(pad_stored, 32)

    @block.gpsimd
    def _(pool):
        nc.gpsimd.memset(ident[:, :], 0.0).then_inc(ident_zero, 1)
        pool.wait_ge(ident_zero, 1)
        nc.gpsimd.affine_select(out=ident[:, :], in_=ident[:, :], compare_op=ALU.not_equal, fill=1.0, base=0,
                                pattern=[[-1, P]], channel_multiplier=1).then_inc(ident_made, 1)
        nc.gpsimd.memset(minus_half[:, :], -0.5).then_inc(ident_zero, 1)
        pool.wait_ge(ident_zero, 2)

        def inverse_sigma(made, count, mean_var, out):
            nc.gpsimd.tensor_scalar(var_e[:, :], mean_var[:, 1:2], EPS, None, ALU.add).then_inc(rstd_step, 1)
            pool.wait_ge(rstd_step, count * 2 + 1)
            nc.gpsimd.tensor_tensor(out[:, 0:1], var_e[:, :], minus_half[:, :], ALU.pow).then_inc(rstd_step, 1)
            pool.wait_ge(rstd_step, count * 2 + 2)
            pool.sem_inc(pool_passed, 1)
            nc.gpsimd.tensor_scalar(out[:, 1:2], mean_var[:, 0:1], out[:, 0:1], -1.0, ALU.mult,
                                    ALU.mult).then_inc(made, 1)

        def queries(i, p, calls):
            pool.wait_ge(stats_made, 2 * i + p + 1)
            pool.sem_inc(pool_passed, 1)
            inverse_sigma(rstd_made, calls, mv[p], rstd[p])
            pool.wait_ge(rstd_made, 2 * i + p + 1)
            pool.wait_ge(khi_made, 2 * i + p + 1)
            nc.gpsimd.tensor_tensor(k_hl[p][DH:P, :], kd[p][DH:P, :], k_hl[p][DH:P, :].bitcast(F32),
                                    ALU.subtract).then_inc(klo_made, 1)
            pool.wait_ge(klo_made, 2 * i + p + 1)
            pool.sem_inc(pool_passed, 1)
            nc.gpsimd.tensor_scalar(q_f[:, :], xd[p][0:DH, :], rstd[p][0:DH, 0:1], rstd[p][0:DH, 1:2], ALU.mult,
                                    ALU.add).then_inc(qf_made, 1)
            pool.wait_ge(qhi_made, 2 * i + p + 1)
            pool.wait_ge(qf_made, 2 * i + p + 1)
            nc.gpsimd.tensor_tensor(q_lo[p][0:DH, :], q_f[:, :], q_hi[p][0:DH, :].bitcast(F32),
                                    ALU.subtract).then_inc(qlo_made, 1)
            pool.wait_ge(klo_made, 2 * i + p + 1)
            pool.wait_ge(qlo_made, 2 * i + p + 1)
            pool.sem_inc(pool_passed, 1)

        def add_attention(i):
            pool.wait_ge(attn_made, i + 1)
            nc.gpsimd.tensor_tensor(x1[:, i, :], x1[:, i, :], attn[:, :], ALU.add).then_inc(x1_made, 1)
            pool.wait_ge(x1_made, i + 1)
            pool.sem_inc(pool_passed, 1)

        def tile_sigma(t, calls):
            if not isinstance(t, int) or t >= 1:
                pool.wait_ge(xhat_made, t)
            pool.wait_ge(stats2_made, t + 1)
            pool.sem_inc(pool_passed, 1)
            inverse_sigma(rstd2_made, calls, mv2, rstd2)

        for n in range(3):
            queries(n // 2, n % 2, n)

        def pair(i, calls):
            later = within(i, 0, 3)
            if later:
                queries(i + 1, 1, calls)
            if isinstance(i, int) and i == 1:
                pool.wait_ge(x1_landed, 32)
            if not isinstance(i, int) or i >= 1:
                add_attention(i - 1)
            if within(i, 0, 4):
                queries(i + 2, 0, calls + 1)
            if not isinstance(i, int) or i >= 1:
                tile_sigma(i - 1, calls + 2 if within(i, 0, 4) else calls + 1 if later else calls)

        pair(0, 3)
        pair(1, 5)
        with pool.Fori(2, NT - 2) as i:
            pair(i, i * 3 + 2)
        calls = (NT - 2) * 3 + 2
        pair(NT - 2, calls)
        pair(NT - 1, calls + 2)
        add_attention(NT - 1)
        tile_sigma(NT - 1, calls + 3)

    @block.scalar
    def _(act):
        def highs(i, p):
            act.wait_ge(k_landed[p], 32 * (i + 1))
            if not isinstance(i, int) or i >= 1:
                act.wait_ge(s_ready, 2 * (2 * i + p - 1))
            nc.scalar.activation(k_hl[p][:, :], kd[p][:, :], ACT.Copy).then_inc(khi_made, 1)
            act.wait_ge(rstd_made, 2 * i + p + 1)
            act.wait_ge(x_landed[p], 32 * (i + 1))
            nc.scalar.activation(q_hi[p][:, :], xd[p][:, :], ACT.Identity, scale=rstd[p][:, 0:1],
                                 bias=rstd[p][:, 1:2]).then_inc(qhi_made, 1)
            nc.scalar.activation(k_h1[p][0:DH, :], kd[p][0:DH, :], ACT.Copy).then_inc(kh1_made, 1)

        def max_row(i, p):
            act.wait_ge(row_ready, 2 * i + p + 1)
            nc.scalar.activation(q_lo[p][DH:DH + 1, :], ps_max[DH:DH + 1, 0, :], ACT.Copy).then_inc(row_made, 1)

        def exponents(i, p):
            if not isinstance(i, int) or i >= 1:
                act.wait_ge(pv_done, 2 * i + p - 1)
            for half in range(2):
                c = slice(half * KC // 2, (half + 1) * KC // 2)
                act.wait_ge(s_ready, 2 * (2 * i + p) + half + 1)
                act.sem_inc(act_passed, 1)
                nc.scalar.activation(probs[p][:, c, :], ps_s[:, c, :], ACT.Exp,
                                     scale=s_pair[:, bass.ts(i, 1)]).then_inc(exp_done, 1)

        def numerators(i, p):
            act.wait_ge(pv_done, 2 * i + p + 1)
            if not isinstance(i, int) or i >= 1:
                act.wait_ge(attn_made, i)
            rows = head_rows[p]
            nc.scalar.activation(numer[rows, :], ps_o[p][rows, :], ACT.Copy).then_inc(numer_made, 1)

        def tile_norm(t, b):
            act.wait_ge(rstd2_made, t + 1)
            if not isinstance(t, int) or t >= 1 and b < 2:
                act.wait_ge(xhat_stored, 16 * t)
                act.wait_ge(blocks_landed, 64 * t)
            nc.scalar.activation(x_hat[b][:, :], x1[:, bass.ts(t, 1), :].rearrange("p o l -> p (o l)"), ACT.Identity,
                                 scale=rstd2[:, 0:1], bias=rstd2[:, 1:2]).then_inc(xhat_made, 1)

        def tile_copy(t):
            act.wait_ge(blocks_turned, t + 1)
            nc.scalar.activation(xt[:, :, bass.ts(t, P)], x_turned[:, :, :], ACT.Copy).then_inc(xt_made, 1)

        def step(i, p, b):
            if within(i, p, -1):
                numerators(*((i - 1, 1) if p == 0 else (i, 0)))
            if within(i, p, 1):
                exponents(*((i, 1) if p == 0 else (i + 1, 0)))
            if within(i, p, 3):
                highs(*((i + 1, 1) if p == 0 else (i + 2, 0)))
            if within(i, p, 2):
                max_row(i + 1, p)
            if p == 0 and within(i, p, -4):
                tile_norm(i - 2, b)
            if p and within(i, p, -7):
                tile_copy(i - 3)

        def weights_high(part):
            act.wait_ge(w_landed[part], part_sum(part))
            split_high(nc, weights, part, 0, whi_made)

        act.wait_ge(consts_made, 1)
        highs(0, 0)
        act.wait_ge(len_cast, 1)
        nc.scalar.activation(len_ln[:, :], len_f[:, :], ACT.Ln).then_inc(len_logged, 1)
        highs(0, 1)
        act.wait_ge(gate_turned, 1)
        nc.scalar.activation(gate_t[:, :, :], ps_o[1][:, 0:KC * E].rearrange("p (c e) -> p c e", c=KC),
                             ACT.Copy).then_inc(gate_made, 1)
        max_row(0, 0)
        act.wait_ge(scale_made, 1)
        exponents(0, 0)
        highs(1, 0)
        max_row(0, 1)
        for i in range(4):
            step(i, 0, i % 2)
            step(i, 1, i % 2)
        with act.Fori(0, (NT - 6) // 2) as k:
            for b in range(2):
                step(k * 2 + (4 + b), 0, b)
                step(k * 2 + (4 + b), 1, b)
        step(NT - 2, 0, 0)
        step(NT - 2, 1, 0)
        weights_high(0)
        step(NT - 1, 0, 1)
        weights_high(1)
        step(NT - 1, 1, 1)
        numerators(NT - 1, 1)
        weights_high(2)
        tile_norm(NT - 2, 0)

        def logits(q):
            act.wait_ge(logits_ready, q + 1)
            nc.scalar.activation(logits_t[:, bass.ts(q, L)], ps_max[0:E, q % 2, :], ACT.Copy).then_inc(logits_made, 1)

        logits(0)
        tile_copy(NT - 3)
        tile_norm(NT - 1, 2)
        tile_copy(NT - 2)
        for q in range(1, dims["early_logits"]):
            logits(q)
        tile_copy(NT - 1)

    @block.vector
    def _(dve):
        nc.vector.memset(zeros_f[:, :], 0.0).then_inc(consts_made, 1)
        nc.vector.memset(ones_f[:, :], 1.0)
        for b in range(2):
            last = nc.vector.memset(v_t[b][:, :, 1, :], 1.0)
        last.then_inc(consts_made, 1)
        dve.wait_ge(consts_made, 2)
        nc.vector.tensor_copy(ones_r[:, :], ones_f[:, :])
        for p in range(2):
            nc.vector.tensor_copy(q_lo[p][DH:96, :], zeros_f[DH:96, :])
            nc.vector.tensor_copy(k_h1[p][DH:96, :], zeros_f[DH:96, :]).then_inc(consts_made, 1)
        dve.wait_ge(consts_made, 4)
        for p in range(2):
            nc.vector.tensor_scalar(k_h1[p][DH:DH + 1, :], zeros_f[DH:DH + 1, :], 1.0, None,
                                    ALU.add).then_inc(consts_made, 1)
        dve.wait_ge(ident_made, 1)
        nc.vector.tensor_scalar(neg_ident[:, :], ident[:, :], -1.0, None, ALU.mult).then_inc(consts_made, 1)

        def head_stats(i, p):
            dve.wait_ge(x_landed[p], 32 * (i + 1))
            nc.vector.bn_stats(stats[p][:, :], xd[p][:, :]).then_inc(stats_raw, 1)
            if not isinstance(i, int) or i >= 1:
                dve.wait_ge(rstd_made, 2 * i + p - 1)
            dve.wait_ge(stats_raw, 2 * i + p + 1)
            dve.sem_inc(dve_passed, 1)
            nc.vector.bn_aggr(mv[p][:, :], stats[p][:, :]).then_inc(stats_made, 1)

        def values(i, b, turns):
            dve.wait_ge(rows_landed[b], 64 * (turns + 1))
            if not isinstance(i, int) or i >= 2:
                dve.wait_ge(pv_done, 2 * i - 2)
            for p in range(2):
                last = nc.vector.transpose(v_t[b][:, :, 2 * p, :].rearrange("p c (g j) -> p g c j", g=2),
                                           k_rows[b][:, 2 * p:2 * p + 2, :].rearrange("p g (j c) -> p g c j", c=KC))
            last.then_inc(v_made, 1)

        def take_max(i, p, half):
            dve.wait_ge(max_ready, 2 * (2 * i + p) + half + 1)
            nc.vector.tensor_reduce(qmax[p][:, 2 * half:2 * half + 2], ps_max[:, :, :], AX.X,
                                    ALU.max).then_inc(max_taken, 1)

        def spread_max(i, p):
            dve.wait_ge(max_taken, 2 * (2 * i + p) + 2)
            if not isinstance(i, int) or i >= 1 or p:
                dve.wait_ge(row_ready, 2 * i + p)
            nc.vector.tensor_tensor(diag[:, :, :], neg_ident[:, :].unsqueeze(1).to_broadcast([P, KC, P]),
                                    qmax[p][:, :].unsqueeze(2).to_broadcast([P, KC, P]),
                                    ALU.mult).then_inc(diag_made, 1)

        def turn_sums(i, p):
            dve.wait_ge(pv_done, 2 * i + p + 1)
            if not isinstance(i, int) or i >= 1:
                dve.wait_ge(recip_made, 2 * i - 1)
            nc.vector.transpose(sums_t[head_rows[p], :], ps_o[p][head_rows[1 - p], :]).then_inc(sums_turned, 1)

        def normalize(i):
            dve.wait_ge(sums_turned, 2 * i + 2)
            nc.vector.reciprocal(recip_col[:, :],
                                 sums_t[:, :].rearrange("p (b c) -> p b c", c=32)[:, :, 0]).then_inc(recip_made, 1)
            dve.wait_ge(recip_made, 2 * i + 1)
            nc.vector.transpose(recip[:, :],
                                recip_col[:, :].unsqueeze(2).to_broadcast([P, L // 32, 32])).then_inc(recip_made, 1)
            dve.wait_ge(recip_made, 2 * i + 2)
            dve.wait_ge(numer_made, 2 * i + 2)
            if not isinstance(i, int) or i >= 1:
                dve.wait_ge(x1_made, i)
            nc.vector.tensor_tensor(attn[:, :], numer[:, :], recip[:, :], ALU.mult).then_inc(attn_made, 1)

        def tile_stats(t):
            dve.wait_ge(x1_made, t + 1)
            if not isinstance(t, int) or t >= 1:
                dve.wait_ge(rstd2_made, t)
            nc.vector.bn_stats(stats2[:, :], x1[:, t, :]).then_inc(stats2_raw, 1)
            dve.wait_ge(stats2_raw, t + 1)
            dve.sem_inc(dve_passed, 1)
            nc.vector.bn_aggr(mv2[:, :], stats2[:, :]).then_inc(stats2_made, 1)

        def tile_turn(t, b):
            if isinstance(t, int) and t == NT - 1:
                dve.wait_ge(last_landed, 64)
            else:
                dve.wait_ge(blocks_landed, 64 * (t + 1))
            if not isinstance(t, int) or t >= 1:
                dve.wait_ge(xt_made, t)
            turn_blocks(nc, x_turned[:, :, :], x_blocks[b]).then_inc(blocks_turned, 1)

        head_stats(0, 0)
        head_stats(0, 1)
        dve.wait_ge(len_landed, 16)
        nc.vector.tensor_copy(len_f[:, :], len_i[:, :]).then_inc(len_cast, 1)
        take_max(0, 0, 0)
        take_max(0, 0, 1)
        spread_max(0, 0)
        dve.wait_ge(len_logged, 1)
        nc.vector.tensor_scalar(s_pair[:, :].rearrange("p (b h) -> p b h", b=B),
                                len_ln[:, :].unsqueeze(2).to_broadcast([P, B, HEADS // 2]), SCALE, None,
                                ALU.mult).then_inc(scale_made, 1)
        values(0, 0, 0)
        head_stats(1, 0)
        take_max(0, 1, 0)
        take_max(0, 1, 1)
        spread_max(0, 1)

        def step(i, p, b, turns):
            if within(i, p, -1):
                turn_sums(*((i - 1, 1) if p == 0 else (i, 0)))
            if within(i, p, 2):
                take_max(i + 1, p, 0)
            if within(i, p, 3):
                head_stats(*((i + 1, 1) if p == 0 else (i + 2, 0)))
            if within(i, p, 2):
                take_max(i + 1, p, 1)
                spread_max(i + 1, p)
            if p == 0 and within(i, p, -1):
                normalize(i - 1)
            if p and within(i, p, -2):
                tile_stats(i - 1)
            if p and within(i, p, -7):
                tile_turn(i - 3, 1 - b)
            if p and within(i, p, 1):
                values(i + 1, 1 - b, turns + b)

        for i in range(4):
            step(i, 0, i % 2, i // 2)
            step(i, 1, i % 2, i // 2)
        with dve.Fori(0, (NT - 6) // 2) as k:
            for b in range(2):
                step(k * 2 + (4 + b), 0, b, k + 2)
                step(k * 2 + (4 + b), 1, b, k + 2)
        def weights_low(part):
            dve.wait_ge(whi_made, part + 1)
            split_low(nc, weights, part, 0, wlo_made)

        step(NT - 2, 0, 0, NT // 2 - 1)
        step(NT - 2, 1, 0, NT // 2 - 1)
        step(NT - 1, 0, 1, NT // 2 - 1)
        weights_low(0)
        step(NT - 1, 1, 1, NT // 2 - 1)
        turn_sums(NT - 1, 1)
        normalize(NT - 1)
        weights_low(1)
        tile_turn(NT - 3, 1)
        tile_stats(NT - 1)
        tile_turn(NT - 2, 0)
        dve.wait_ge(whi_made, 4)
        weights_low(2)
        tile_turn(NT - 1, 1)

    @block.tensor
    def _(pe):
        def max_scores(i, p, half):
            pe.wait_ge(klo_made, 2 * i + p + 1)
            pe.wait_ge(qhi_made, 2 * i + p + 1)
            if half or p or not isinstance(i, int) or i >= 1:
                pe.wait_ge(max_taken, 2 * (2 * i + p) + half)
            if half == 0 and (p or not isinstance(i, int) or i >= 1):
                pe.wait_ge(row_made, 2 * i + p)
            for j in range(2):
                last = nc.tensor.matmul(ps_max[:, j, :], q_hi[p][:, bass.ts(2 * half + j, P)], k_hl[p][:, :],
                                        start=True, stop=True)
            last.then_inc(max_ready, 1)

        def spread_row(i, p):
            pe.wait_ge(diag_made, 2 * i + p + 1)
            nc.tensor.matmul(ps_max[:, 0, :], ones_r[:, :], diag[:, :, :], start=True,
                             stop=True).then_inc(row_ready, 1)

        def chunk_keys(k, c, rows):
            return k[0:rows, c:L:KC]

        def scores_high(i, p):
            if p or not isinstance(i, int) or i >= 1:
                pe.wait_ge(exp_done, 2 * (2 * i + p))
            for c in range(KC):
                nc.tensor.matmul(ps_s[:, c, :], chunk_keys(k_hl[p], c, P), q_hi[p][:, :], start=True, stop=False)

        def scores_low(i, p):
            pe.wait_ge(row_made, 2 * i + p + 1)
            pe.wait_ge(kh1_made, 2 * i + p + 1)
            pe.wait_ge(qlo_made, 2 * i + p + 1)
            for c in range(KC):
                last = nc.tensor.matmul(ps_s[:, c, :], chunk_keys(k_h1[p], c, 96), q_lo[p][0:96, :],
                                        start=False, stop=True)
                if c % 2:
                    last.then_inc(s_ready, 1)

        def weigh_values(i, p, b, chunks):
            for c in chunks:
                if c == 0:
                    pe.wait_ge(v_made, i + 1)
                    if not isinstance(i, int) or i >= 1:
                        pe.wait_ge(numer_made, 2 * i + p - 1)
                        pe.wait_ge(sums_turned, 2 * i + p - 1)
                    elif p:
                        pe.wait_ge(gate_made, 1)
                if c % 2 == 0:
                    pe.wait_ge(exp_done, 2 * (2 * i + p) + c // 2 + 1)
                last = nc.tensor.matmul(ps_o[p][:, :], v_t[b][:, c, p:p + 2, :], probs[p][:, c, :], start=c == 0,
                                        stop=c == KC - 1)
            if KC - 1 in chunks:
                last.then_inc(pv_done, 1)

        def step(i, p, b, turns):
            following = (i, 1) if p == 0 else (i + 1, 0)
            if within(i, p, 1):
                scores_high(*following)
            if within(i, p, 2):
                max_scores(i + 1, p, 0)
            if within(i, p, 1):
                scores_low(*following)
            weigh_values(i, p, b, [0])
            if within(i, p, 2):
                max_scores(i + 1, p, 1)
            weigh_values(i, p, b, [1, 2, 3])
            if within(i, p, 2):
                spread_row(i + 1, p)

        pe.wait_ge(ident_made, 1)
        pe.wait_ge(consts_made, 7)
        max_scores(0, 0, 0)
        pe.wait_ge(gate_landed, 16)
        for c in range(KC):
            last = nc.tensor.transpose(ps_o[1][:, c * E:(c + 1) * E], gate_sb[:, c:L:KC], ident[0:E, 0:E])
        last.then_inc(gate_turned, 1)
        max_scores(0, 0, 1)
        spread_row(0, 0)
        scores_high(0, 0)
        max_scores(0, 1, 0)
        scores_low(0, 0)
        max_scores(0, 1, 1)
        spread_row(0, 1)
        for i in range(4):
            step(i, 0, i % 2, i // 2)
            step(i, 1, i % 2, i // 2)
        with pe.Fori(0, (NT - 6) // 2) as k:
            for b in range(2):
                step(k * 2 + (4 + b), 0, b, k + 2)
                step(k * 2 + (4 + b), 1, b, k + 2)
        for i in range(NT - 2, NT):
            step(i, 0, i % 2, i // 2)
            step(i, 1, i % 2, i // 2)
        pe.wait_ge(row_made, NH)
        for q in range(dims["early_logits"]):
            pe.wait_ge(xt_made, (q + 1) * (L // P))
            if q >= 2:
                pe.wait_ge(logits_made, q - 1)
            for c in range(KC):
                last = nc.tensor.matmul(ps_max[0:E, q % 2, :], gate_t[:, c, :], xt[:, c, bass.ts(q, L)], start=c == 0,
                                        stop=c == KC - 1)
            last.then_inc(logits_ready, 1)


def experts_block(nc, ctx, dims, dram, keep):
    T, L, E, H = dims["T"], dims["L"], dims["E"], dims["H"]
    NT = T // P
    GROUP = 2 * P
    NS = T // GROUP
    NX = 2 * T // GROUP + E - 1
    KC = L // P
    MH = -(-H // P)
    HR = [min(P, H - m * P) for m in range(MH)]
    assert NS == 8 and NX % 2 == 1 and KC == 4 and MH == 3 and E == 8

    def sb(name, shape, dt=F32):
        return ctx.enter_context(nc.sbuf_tensor(name, shape, dt))

    def ps(name, shape, dt=F32):
        return ctx.enter_context(nc.psum_tensor(name, shape, dt))

    def sem(name):
        return ctx.enter_context(nc.semaphore(name))

    x1, xt, ident, ones_f = keep["x1"], keep["xt"], keep["ident"], keep["ones_f"]
    gate_t, logits_t, x_rows, weights = keep["gate_t"], keep["logits_t"], keep["x_rows"], keep["weights"]

    for half in ("hi", "lo"):
        weights[half].append([sb(f"w{n}_{half}1", [P, c, f], F32R)
                              for n, c, f in ((1, KC, H), (3, KC, H), (2, MH, L))])
    w_hi, w_lo = weights["hi"], weights["lo"]
    x_hi = [sb(f"x_hi{b}", [P, KC, GROUP], F32R) for b in range(2)]
    x_lo = [sb(f"x_lo{b}", [P, KC, GROUP], F32R) for b in range(2)]
    silu = sb("silu", [P, MH, GROUP])
    g_f = sb("g_f", [P, MH, GROUP])
    g_hi = sb("g_hi", [P, MH, GROUP], F32R)
    g_lo = sb("g_lo", [P, MH, GROUP], F32R)
    y_sb = [sb(f"y_sb{j}", [P, L]) for j in range(2)]
    x_blocks = [xt[:, b, 0:2 * L].rearrange("p (j q f) -> p j q f", j=2, q=4) for b in range(2)]
    x_turned = [xt[:, 2 + b, 0:KC * GROUP].rearrange("p (c t) -> p c t", c=KC) for b in range(2)]
    slots_in = [sb(f"slots_in{p}", [P, 2, 2], U32) for p in range(2)]
    slots_out = [sb(f"slots_out{p}", [P, 2, 2], U32) for p in range(2)]

    e_neg = sb("e_neg", [P, NT, E])
    score = sb("score", [P, NT, E])
    top = sb("top", [P, NT, 8])
    top_i = sb("top_i", [P, NT, 8], U32)
    top_f = sb("top_f", [P, NT, 2])
    iota_e = sb("iota_e", [P, E])
    chosen = [sb(f"chosen{j}", [P, NT, E]) for j in range(2)]
    either = sb("either", [P, NT, E], BF16)
    top_sum = sb("top_sum", [P, NT])
    top_inv = sb("top_inv", [P, NT])
    upper = sb("upper", [P, P], BF16)
    ones_b = sb("ones_b", [P, P], BF16)
    running = sb("running", [P, E, NT])
    before = sb("before", [P, E])
    count = sb("count", [P, E])
    need = sb("need", [P, E])
    need_up = sb("need_up", [P, E])
    ends = sb("ends", [P, E])
    starts = sb("starts", [P, E])
    place_a = sb("place_a", [P, E, NT])
    picked = sb("picked", [P, NT, E])
    dest_f = sb("dest_f", [P, 2, NT])
    dest = sb("dest", [P, 2, NT], U32)
    entry = sb("entry", [P, NT, 2, 2], U32)
    iota_g = sb("iota_g", [1, NX + 1])
    past = sb("past", [1, NX + 1, E])
    group_f = sb("group_f", [1, NX + 1])
    group_e = sb("group_e", [1, NX + 1], I32)
    table = sb("table", [P, 2 * NX, 2], U32)

    ps_h = [ps(f"ps_h{m}", [P, 2, GROUP]) for m in range(MH)]
    ps_y = [ps(f"ps_y{j}", [P, L]) for j in range(2)]
    ps_r = ps("ps_r", [P, 4, P])

    names = """logits_ready logits_made logits_turned exp_made score_step
        top_made entry_iota iota_made either_made ranks_ready route_step dest_made group_made consts_set upper_zero
        upper_made table_preset table_filled table_landed xhi_made xlo_made hu_ready silu_made gf_made ghi_made
        glo_made y_ready y_taken out_stored upper_hi_made upper_lo_made lower_hi_made lower_lo_made ins_made outs_made
        turned add_done w1_landed w3_landed w2_landed entry_made gather_passed sp_passed""".split()
    S = {n: sem(n) for n in names}
    x_landed = [sem(f"rows_landed{p}") for p in range(2)]
    blocks_landed = [sem(f"blocks_landed{p}") for p in range(2)]
    w_landed = [S["w1_landed"], S["w3_landed"], S["w2_landed"]]

    out, xn, slot_table = dram["out"], dram["xn"], dram["slots"]
    block = ctx.enter_context(nc.Block("experts"))

    LAST = NS + NX - 1

    def at_least(v, bound):
        return not isinstance(v, int) or v >= bound

    def at_most(v, bound):
        return not isinstance(v, int) or v <= bound

    def run(eng, step, between=None):
        for G in range(2):
            step(G, G)
            if between is not None and G == 0:
                between()
        with eng.Fori(1, (NS - 2) // 2) as k:
            for b in range(2):
                step(k * 2 + b, b)
        for G in range(NS - 2, NS + 2):
            step(G, G % 2, G - NS, (G - NS) // 2)
        with eng.Fori(1, (NX - 3) // 2) as k:
            for b in range(2):
                step(k * 2 + (NS + b), b, k * 2 + b, k)
        for G in range(LAST - 2, LAST + 1):
            step(G, G % 2, G - NS, (G - NS) // 2)

    @block.sync
    def _(sp):
        def load(k, w, parts):
            for part in parts:
                if k is not None and at_least(k, 2):
                    if part < 2:
                        sp.wait_ge(S["upper_lo_made"], 2 * k - 3 + part)
                    else:
                        sp.wait_ge(S["lower_lo_made"], 2 * k - 2)
                load_part(sp, weights, part, w[part], w_landed[part])

        def load_group(s, parts):
            e = sp.value_load(group_e[0:1, bass.ds(s, 1)], min_val=0, max_val=E - 1)
            load(s + 1, [dram["w1"][e], dram["w3"][e], dram["w2"][e]], parts)

        def store(t):
            sp.wait_ge(S["y_taken"], t + 1)
            sp.dma_start(out[bass.ts(t, P), :], x1[:, t, :]).then_inc(S["out_stored"], 16)

        def spread(s, h, p):
            sp.wait_ge(x_landed[p], 32 * (h + 1))
            if at_least(s, 2):
                sp.wait_ge(S["turned"], 2 * (s - 1))
            else:
                sp.wait_ge(S["xlo_made"], 2 * NS)
            if not isinstance(s, int):
                sp.sem_inc(S["sp_passed"], 1)
            for j in range(2):
                spread_blocks(sp, x_blocks[p][:, j], x_rows[:, 2 * p + j, :], blocks_landed[p])

        with sp.Fori(0, NS - 2) as t:
            store(t)
        sp.wait_ge(S["group_made"], 1)
        load_group(0, (0, 1, 2))
        for t in range(NS - 2, 2 * NS - 4):
            store(t)
        spread(0, 0, 0)
        spread(1, 0, 1)
        load_group(1, (0, 1))
        for t in range(2 * NS - 4, 2 * NS - 2):
            store(t)
        load_group(2, (0, 1))
        spread(2, 1, 0)
        for t in range(2 * NS - 2, 2 * NS):
            store(t)
        load_group(1, (2,))
        with sp.Fori(0, (NX - 3) // 2) as k:
            for u in range(2):
                s = k * 2 + (3 + u)
                load_group(s, (0, 1))
                spread(s, k + (1 + u), 1 - u)
                load_group(k * 2 + (2 + u), (2,))
        load_group(NX - 1, (2,))

    @block.gpsimd
    def _(pool):
        nc.gpsimd.memset(upper[:, :], 1.0).then_inc(S["upper_zero"], 1)
        pool.wait_ge(S["upper_zero"], 1)
        nc.gpsimd.affine_select(out=upper[:, :], in_=upper[:, :], compare_op=ALU.is_gt, fill=0.0, base=0,
                                pattern=[[1, P]], channel_multiplier=-1).then_inc(S["upper_made"], 1)
        nc.gpsimd.iota(iota_e[:, :], [[1, E]], base=0, channel_multiplier=0,
                       allow_small_or_imprecise_dtypes=True).then_inc(S["iota_made"], 1)
        nc.gpsimd.iota(iota_g[:, :], [[1, NX + 1]], base=0, channel_multiplier=0,
                       allow_small_or_imprecise_dtypes=True).then_inc(S["iota_made"], 1)
        nc.gpsimd.iota(entry[:, :, :, 0], [[P, NT], [0, 2]], base=0, channel_multiplier=1).then_inc(S["entry_iota"], 1)
        nc.gpsimd.iota(table[:, :, 0], [[0, 2 * NX]], base=T, channel_multiplier=1).then_inc(S["entry_iota"], 1)
        nc.gpsimd.iota(table[:, :, 1], [[0, 2 * NX]], base=0, channel_multiplier=0).then_inc(S["entry_iota"], 1)
        pool.wait_ge(S["entry_iota"], 3)
        table_dram = slot_table.rearrange("(g p) w -> p g w", p=P)
        pool.dma_start(table_dram, table[:, :, :]).then_inc(S["table_preset"], 16)
        pool.wait_ge(S["table_preset"], 16)
        pool.wait_ge(S["dest_made"], 1)
        pool.wait_ge(S["entry_made"], 1)
        for i in range(NT):
            for j in range(2):
                nc.gpsimd.indirect_dma_start(
                    slot_table, bass.IndirectOffsetOnAxis(ap=dest[:, j, i:i + 1], axis=0), entry[:, i, j, :],
                    None).then_inc(S["table_filled"], 16)
        pool.wait_ge(S["table_filled"], 16 * 2 * NT)
        pool.dma_start(table[:, :, :], table_dram).then_inc(S["table_landed"], 16)
        pool.wait_ge(S["table_landed"], 16)

        def slots_for(s, slots, made):
            if not isinstance(s, int):
                pool.sem_inc(S["gather_passed"], 1)
            nc.gpsimd.tensor_copy(slots[:, :, :], table[:, bass.ts(s, 2), :]).then_inc(made, 1)

        def fetch(s, h, p):
            if at_least(s, 2):
                pool.wait_ge(blocks_landed[p], 128 * h)
            slots_for(s, slots_in[p], S["ins_made"])
            pool.wait_ge(S["ins_made"], s + 1)
            pool.sem_inc(S["gather_passed"], 1)
            for j in range(2):
                nc.gpsimd.indirect_dma_start(
                    x_rows[:, 2 * p + j, :], None, xn,
                    bass.IndirectOffsetOnAxis(ap=slots_in[p][:, j, 0:1], axis=0)).then_inc(x_landed[p], 16)

        def add(s, p):
            for j in range(2):
                pool.wait_ge(S["y_taken"], 2 * (NS + s) + j + 1)
                if j or at_least(s, 1):
                    pool.wait_ge(S["add_done"], 16 * (2 * s + j))
                pool.sem_inc(S["gather_passed"], 1)
                nc.gpsimd.indirect_dma_start(
                    out, bass.IndirectOffsetOnAxis(ap=slots_out[p][:, j, 0:1], axis=0), y_sb[j][:, :], None,
                    compute_op=ALU.add).then_inc(S["add_done"], 16)

        def step(s, p, h):
            add(s, p)
            if at_most(s, NX - 5):
                fetch(s + 4, h + 2, p)
            if at_most(s, NX - 3):
                pool.wait_ge(S["add_done"], 32 * (s + 1))
                slots_for(s + 2, slots_out[p], S["outs_made"])

        for s in range(2):
            fetch(s, 0, s)
            slots_for(s, slots_out[s], S["outs_made"])
        for s in range(2):
            fetch(s + 2, 1, s)
        pool.wait_ge(S["out_stored"], 16 * 2 * NS)
        for s in range(2):
            step(s, s, 0)
        with pool.Fori(1, (NX - 5) // 2) as k:
            for p in range(2):
                step(k * 2 + p, p, k)
        for s in range(NX - 5, NX):
            step(s, s % 2, s // 2)
        pool.wait_ge(S["add_done"], 32 * NX)

    @block.scalar
    def _(act):
        def split_x(G, b, j, s=None):
            if at_least(G, 2):
                act.wait_ge(S["hu_ready"], 3 * (G - 1))
            if s is None:
                source = xt[:, :, bass.ds(G * GROUP + j * P, P)]
            else:
                act.wait_ge(S["turned"], 2 * s + j + 1)
                source = x_turned[b][:, :, bass.ts(j, P)]
            nc.scalar.activation(x_hi[b][:, :, bass.ts(j, P)], source, ACT.Copy).then_inc(S["xhi_made"], 1)

        def gate(G, m):
            act.wait_ge(S["hu_ready"], 3 * G + m + 1)
            if at_least(G, 1):
                act.wait_ge(S["gf_made"], 3 * G + m - 2)
            nc.scalar.activation(silu[0:HR[m], m, :], ps_h[m][0:HR[m], 0, :], ACT.Silu).then_inc(S["silu_made"], 1)

        def weight_y(G, s, p):
            for j in range(2):
                act.wait_ge(S["y_ready"], 2 * G + j + 1)
                act.wait_ge(S["outs_made"], s + 1)
                if at_least(s, 1):
                    act.wait_ge(S["add_done"], 16 * (2 * s - 1 + j))
                nc.scalar.activation(y_sb[j][:, :], ps_y[j][:, :], ACT.Copy,
                                     scale=slots_out[p][:, j, 1:2].bitcast(F32)).then_inc(S["y_taken"], 1)

        def upper_high(k, p, part):
            act.wait_ge(S["hu_ready"], 3 * (k + (NS - 2)))
            act.wait_ge(w_landed[part], 16 * k)
            split_high(nc, weights, part, p, S["upper_hi_made"])

        def lower_high(k, p):
            act.wait_ge(S["y_ready"], 2 * (k + (NS - 2)))
            act.wait_ge(w_landed[2], 32 * k)
            split_high(nc, weights, 2, p, S["lower_hi_made"])

        for G in range(2):
            for j in range(2):
                split_x(G, G, j)
        for n, q in enumerate(range(dims["early_logits"], T // L)):
            act.wait_ge(S["logits_ready"], n + 1)
            nc.scalar.activation(logits_t[:, bass.ts(q, L)], ps_y[n % 2][0:E, :], ACT.Copy).then_inc(S["logits_made"], 1)
        act.wait_ge(S["logits_turned"], 1)
        nc.scalar.activation(e_neg[:, :, :], ps_r[:, 0, :].rearrange("p (i e) -> p i e", e=E), ACT.Exp,
                             scale=-1.0).then_inc(S["exp_made"], 1)
        for m in range(MH):
            gate(0, m)

        def step(G, b, s=None, h=None):
            routed_2 = s is not None and at_least(s, -2) and at_most(s, NX - 3)
            if routed_2:
                upper_high(s + 3, 1 - b, 0)
                upper_high(s + 3, 1 - b, 1)
            if at_most(G, LAST - 1):
                gate(G + 1, 0)
            if s is not None and at_least(s, 0):
                weight_y(G, s, b)
            if s is None:
                for j in range(2):
                    split_x(G + 2, b, j)
            elif routed_2:
                for j in range(2):
                    split_x(G + 2, b, j, s + 2)
            if s is not None and at_least(s, -1) and at_most(s, NX - 2):
                lower_high(s + 2, b)
            if at_most(G, LAST - 1):
                gate(G + 1, 1)
                gate(G + 1, 2)

        run(act, step)

    @block.vector
    def _(dve):
        def split_x(G, b, j, s=None):
            dve.wait_ge(S["xhi_made"], 2 * G + j + 1)
            source = xt[:, :, bass.ds(G * GROUP + j * P, P)] if s is None else x_turned[b][:, :, bass.ts(j, P)]
            nc.vector.tensor_tensor(x_lo[b][:, :, bass.ts(j, P)], source, x_hi[b][:, :, bass.ts(j, P)].bitcast(F32),
                                    ALU.subtract).then_inc(S["xlo_made"], 1)

        def turn(s, h, p):
            dve.wait_ge(blocks_landed[p], 128 * (h + 1))
            for j in range(2):
                turn_blocks(nc, x_turned[p][:, :, bass.ts(j, P)], x_blocks[p][:, j]).then_inc(S["turned"], 1)

        def hidden(G, m):
            r = HR[m]
            dve.wait_ge(S["silu_made"], 3 * G + m + 1)
            nc.vector.tensor_tensor(g_f[0:r, m, :], silu[0:r, m, :], ps_h[m][0:r, 1, :],
                                    ALU.mult).then_inc(S["gf_made"], 1)
            dve.wait_ge(S["gf_made"], 3 * G + m + 1)
            if at_least(G, 1):
                dve.wait_ge(S["y_ready"], 2 * G)
            nc.vector.tensor_copy(g_hi[0:r, m, :], g_f[0:r, m, :]).then_inc(S["ghi_made"], 1)
            dve.wait_ge(S["ghi_made"], 3 * G + m + 1)
            nc.vector.tensor_tensor(g_lo[0:r, m, :], g_f[0:r, m, :], g_hi[0:r, m, :].bitcast(F32),
                                    ALU.subtract).then_inc(S["glo_made"], 1)

        def add_x1(G):
            for j in range(2):
                dve.wait_ge(S["y_ready"], 2 * G + j + 1)
                t = G * 2 + j
                nc.vector.tensor_tensor(x1[:, t, :], ps_y[j][:, :], x1[:, t, :], ALU.add).then_inc(S["y_taken"], 1)

        def upper_low(k, p, part):
            dve.wait_ge(S["upper_hi_made"], 2 * k - 1 + part)
            split_low(nc, weights, part, p, S["upper_lo_made"])

        def lower_low(k, p):
            dve.wait_ge(S["lower_hi_made"], 2 * k)
            split_low(nc, weights, 2, p, S["lower_lo_made"])

        def scores():
            dve.wait_ge(S["exp_made"], 1)
            nc.vector.tensor_scalar(e_neg[:, :, :], e_neg[:, :, :], 1.0, None, ALU.add).then_inc(S["score_step"], 1)
            dve.wait_ge(S["score_step"], 1)
            nc.vector.reciprocal(score[:, :, :], e_neg[:, :, :]).then_inc(S["score_step"], 1)
            dve.wait_ge(S["score_step"], 2)
            for i in range(NT):
                nc.vector.max(top[:, i, :], score[:, i, :]).then_inc(S["top_made"], 1)
            for i in range(NT):
                dve.wait_ge(S["top_made"], i + 1)
                last = nc.vector.max_index(top_i[:, i, :], top[:, i, :], score[:, i, :])
            last.then_inc(S["score_step"], 1)
            dve.wait_ge(S["score_step"], 3)
            nc.vector.tensor_copy(top_f[:, :, :], top_i[:, :, 0:2]).then_inc(S["score_step"], 1)
            dve.wait_ge(S["score_step"], 4)
            dve.wait_ge(S["iota_made"], 2)
            for j in range(2):
                nc.vector.tensor_tensor(chosen[j][:, :, :], iota_e[:, :].unsqueeze(1).to_broadcast([P, NT, E]),
                                        top_f[:, :, j:j + 1].to_broadcast([P, NT, E]),
                                        ALU.is_equal).then_inc(S["score_step"], 1)
            dve.wait_ge(S["score_step"], 6)
            nc.vector.tensor_tensor(either[:, :, :], chosen[0][:, :, :], chosen[1][:, :, :],
                                    ALU.add).then_inc(S["either_made"], 1)
            nc.vector.tensor_tensor(top_sum[:, :], top[:, :, 0], top[:, :, 1], ALU.add).then_inc(S["score_step"], 1)
            dve.wait_ge(S["score_step"], 7)
            nc.vector.tensor_scalar(top_sum[:, :], top_sum[:, :], 1e-20, None, ALU.add).then_inc(S["score_step"], 1)
            dve.wait_ge(S["score_step"], 8)
            nc.vector.reciprocal(top_inv[:, :], top_sum[:, :]).then_inc(S["score_step"], 1)
            dve.wait_ge(S["score_step"], 9)
            for j in range(2):
                nc.vector.scalar_tensor_tensor(entry[:, :, j, 1].bitcast(F32), top[:, :, j], dims["routed_scale"],
                                               top_inv[:, :], ALU.mult, ALU.mult).then_inc(S["score_step"], 1)
            dve.wait_ge(S["score_step"], 11)
            dve.wait_ge(S["entry_iota"], 3)
            dve.sem_inc(S["entry_made"], 1)


        def places():
            ranks = ps_r[:, 1, :].rearrange("p (e i) -> p e i", e=E)
            totals = ps_r[:, 2, :]
            steps = [0]

            def routed(ins):
                steps[0] += 1
                ins.then_inc(S["route_step"], 1)
                dve.wait_ge(S["route_step"], steps[0])

            dve.wait_ge(S["ranks_ready"], 1)
            routed(nc.vector.tensor_tensor_scan(running[:, :, :].rearrange("p e i -> p (e i)"), ones_f[:, 0:E * NT], totals,
                                                0.0, ALU.mult, ALU.add))
            routed(nc.vector.memset(before[:, 0:1], 0.0))
            routed(nc.vector.tensor_copy(before[:, 1:E], running[:, 0:E - 1, NT - 1]))
            routed(nc.vector.tensor_tensor(count[:, :], running[:, :, NT - 1], before[:, :], ALU.subtract))
            routed(nc.vector.tensor_scalar(need[:, :], count[:, :], 1.0 / GROUP, 0.5 - 0.5 / GROUP, ALU.mult, ALU.add))
            routed(nc.vector.tensor_scalar(need_up[:, :], need[:, :], 8388608.0, None, ALU.add))
            routed(nc.vector.tensor_scalar(need[:, :], need_up[:, :], -8388608.0, None, ALU.add))
            routed(nc.vector.tensor_tensor_scan(ends[:, :], ones_f[:, 0:E], need[:, :], 0.0, ALU.mult, ALU.add))
            routed(nc.vector.tensor_tensor(past[:, :, :], ends[0:1, :].unsqueeze(1).to_broadcast([1, NX + 1, E]),
                                           iota_g[:, :].unsqueeze(2).to_broadcast([1, NX + 1, E]), ALU.is_le))
            routed(nc.vector.tensor_reduce(group_f[:, :], past[:, :, :], AX.X, ALU.add))
            nc.vector.tensor_scalar(group_e[:, :], group_f[:, :], float(E - 1), None, ALU.min).then_inc(S["group_made"], 1)
            routed(nc.vector.tensor_tensor(starts[:, :], ends[:, :], need[:, :], ALU.subtract))
            routed(nc.vector.scalar_tensor_tensor(starts[:, :], starts[:, :], float(GROUP), before[:, :], ALU.mult,
                                                  ALU.subtract))
            routed(nc.vector.tensor_tensor(place_a[:, :, :].rearrange("p e i -> p (e i)"),
                                           running[:, :, :].rearrange("p e i -> p (e i)"), totals, ALU.subtract))
            routed(nc.vector.tensor_tensor(place_a[:, :, :], place_a[:, :, :], ranks, ALU.add))
            routed(nc.vector.tensor_tensor(place_a[:, :, :], place_a[:, :, :],
                                           starts[:, :].unsqueeze(2).to_broadcast([P, E, NT]), ALU.add))
            for j in range(2):
                routed(nc.vector.tensor_tensor(picked[:, :, :], chosen[j][:, :, :],
                                               place_a[:, :, :].rearrange("p e i -> p i e"), ALU.mult))
                routed(nc.vector.tensor_reduce(dest_f[:, j, :], picked[:, :, :], AX.X, ALU.add))
            nc.vector.tensor_copy(dest[:, :, :], dest_f[:, :, :]).then_inc(S["dest_made"], 1)


        def step(G, b, s=None, h=None):
            routed_2 = s is not None and at_least(s, -2) and at_most(s, NX - 3)
            if routed_2:
                upper_low(s + 3, 1 - b, 0)
                upper_low(s + 3, 1 - b, 1)
            if routed_2:
                turn(s + 2, h + 1, b)
            if s is None or not at_least(s, 0):
                add_x1(G)
            if at_most(G, LAST - 1):
                hidden(G + 1, 0)
            if s is None:
                for j in range(2):
                    split_x(G + 2, b, j)
            elif routed_2:
                for j in range(2):
                    split_x(G + 2, b, j, s + 2)
            if s is not None and at_least(s, -1) and at_most(s, NX - 2):
                lower_low(s + 2, b)
            if at_most(G, LAST - 1):
                hidden(G + 1, 1)
                hidden(G + 1, 2)

        nc.vector.memset(ones_b[:, :], 1.0).then_inc(S["consts_set"], 1)
        for G in range(2):
            for j in range(2):
                split_x(G, G, j)
        scores()
        for m in range(MH):
            hidden(0, m)
        run(dve, step, places)

    @block.tensor
    def _(pe):
        def up(G, b, tiles, k, p):
            pe.wait_ge(S["xlo_made"], 2 * G + 2)
            if k is not None:
                pe.wait_ge(S["upper_lo_made"], 2 * k)
            for m in tiles:
                cols = slice(m * P, m * P + HR[m])
                if at_least(G, 1):
                    pe.wait_ge(S["gf_made"], 3 * G + m - 2)
                for part in range(2):
                    acc = ps_h[m][0:HR[m], part, :]
                    hi, lo = w_hi[p][part], w_lo[p][part]
                    for c in range(KC):
                        nc.tensor.matmul(acc, hi[:, c, cols], x_hi[b][:, c, :], start=c == 0, stop=False)
                        nc.tensor.matmul(acc, hi[:, c, cols], x_lo[b][:, c, :], start=False, stop=False)
                        last = nc.tensor.matmul(acc, lo[:, c, cols], x_hi[b][:, c, :], start=False, stop=c == KC - 1)
                last.then_inc(S["hu_ready"], 1)

        def down(G, k, p):
            if k is not None:
                pe.wait_ge(S["lower_lo_made"], 2 * k)
            hi, lo = w_hi[p][2], w_lo[p][2]
            for j in range(2):
                if at_least(G, 1):
                    pe.wait_ge(S["y_taken"], 2 * G + j - 1)
                for m in range(MH):
                    pe.wait_ge(S["glo_made"], 3 * G + m + 1)
                    r, tokens = HR[m], bass.ts(j, P)
                    nc.tensor.matmul(ps_y[j][:, :], g_hi[0:r, m, tokens], hi[0:r, m, :], start=m == 0, stop=False)
                    nc.tensor.matmul(ps_y[j][:, :], g_hi[0:r, m, tokens], lo[0:r, m, :], start=False, stop=False)
                    last = nc.tensor.matmul(ps_y[j][:, :], g_lo[0:r, m, tokens], hi[0:r, m, :], start=False,
                                            stop=m == MH - 1)
                last.then_inc(S["y_ready"], 1)

        late = T // L - dims["early_logits"]
        for n, q in enumerate(range(dims["early_logits"], T // L)):
            for c in range(KC):
                last = nc.tensor.matmul(ps_y[n % 2][0:E, :], gate_t[:, c, :], xt[:, c, bass.ts(q, L)], start=c == 0,
                                        stop=c == KC - 1)
            last.then_inc(S["logits_ready"], 1)
        pe.wait_ge(S["logits_made"], late)
        for i in range(NT):
            last = nc.tensor.transpose(ps_r[:, 0, i * E:(i + 1) * E], logits_t[:, bass.ts(i, P)], ident[0:E, 0:E])
        last.then_inc(S["logits_turned"], 1)
        up(0, 0, range(MH), None, 0)

        def count_ranks():
            pe.wait_ge(S["either_made"], 1)
            pe.wait_ge(S["upper_made"], 1)
            pe.wait_ge(S["consts_set"], 1)
            by_expert = either[:, :, :].rearrange("p i e -> p e i")
            nc.tensor.matmul(ps_r[:, 1, :], upper[:, :], by_expert, start=True, stop=True)
            nc.tensor.matmul(ps_r[:, 2, :], ones_b[:, :], by_expert, start=True, stop=True).then_inc(S["ranks_ready"], 1)

        def step(G, b, s=None, h=None):
            routed, routed_1 = s is not None and at_least(s, 0), s is not None and at_least(s, -1)
            set_1 = (s + 2, b) if routed_1 else (None, 0)
            if at_most(G, LAST - 1):
                up(G + 1, 1 - b, [0], *set_1)
            if isinstance(G, int) and G == 0:
                count_ranks()
            down(G, *((s + 1, 1 - b) if routed else (None, 0)))
            if at_most(G, LAST - 1):
                up(G + 1, 1 - b, [1, 2], *set_1)

        run(pe, step)


def build(nc, ins, out):
    x = ins["x"]
    B, C, L = x.shape
    E, _, H = ins["L0_ffn_w1"].shape
    T = B * C
    NT = T // P
    NX = 2 * T // (2 * P) + E - 1
    dims = {"B": B, "C": C, "L": L, "T": T, "E": E, "H": H, "routed_scale": 2.5, "early_logits": 3}
    dram = {
        "x": x, "ctx": ins["ctx_2048"], "lengths": ins["itok_B_779_1933"], "out": out,
        "gate": ins["L0_ffn_gate_w"], "w1": ins["L0_ffn_w1"], "w2": ins["L0_ffn_w2"], "w3": ins["L0_ffn_w3"],
        "sw1": ins["L0_ffn_sw1"], "sw2": ins["L0_ffn_sw2"], "sw3": ins["L0_ffn_sw3"],
        "xn": nc.dram_tensor("xn", (T + P, L), F32, kind="Internal").ap(),
        "slots": nc.dram_tensor("slots", (NX * 2 * P, 2), U32, kind="Internal").ap(),
    }
    with ExitStack() as common:
        def sb(name, shape, dt=F32):
            return common.enter_context(nc.sbuf_tensor(name, shape, dt))

        keep = {"x1": sb("x1", [P, NT, L]), "xt": sb("xt", [P, L // P, T]), "ident": sb("ident", [P, P]),
                "ones_f": sb("ones_f", [P, P]), "gate_t": sb("gate_t", [P, L // P, E])}
        rows = sb("x_rows", [P, 4, L])
        keep["x_rows"] = rows
        keep["logits_t"] = rows[0:E, :, :].rearrange("e q l -> e (q l)")
        KC, MH = L // P, -(-H // P)
        shapes = ((1, KC, H), (3, KC, H), (2, MH, L))
        keep["weights"] = {"f": [sb(f"w{n}_f", [P, c, f]) for n, c, f in shapes], "last_rows": H - (MH - 1) * P}
        for half in ("hi", "lo"):
            keep["weights"][half] = [[sb(f"w{n}_{half}0", [P, c, f], F32R) for n, c, f in shapes]]
        for stage in (attention_block, experts_block):
            with ExitStack() as ctx:
                stage(nc, ctx, dims, dram, keep)


_INS = ['x', 'ctx_2048', 'itok_B_779_1933', 'L0_ffn_gate_w', 'L0_ffn_w1', 'L0_ffn_w2', 'L0_ffn_w3', 'L0_ffn_sw1',
        'L0_ffn_sw2', 'L0_ffn_sw3']


def kernel(**inputs):
    import concourse.bacc as _bacc
    from concourse.bass_utils import run_bass_kernel_spmd as _run

    nc = _bacc.Bacc("TRN2", target_bir_lowering=False, num_devices=1)
    arrays, aps = {}, {}
    for name in _INS:
        a = np.ascontiguousarray(inputs[name])
        arrays[f"in_{name}_dram"] = a
        aps[name] = nc.dram_tensor(f"in_{name}_dram", a.shape, mybir.dt.from_np(a.dtype), kind="ExternalInput").ap()
    shape = inputs["x"].shape
    rows = shape[0] * shape[1]
    out = nc.dram_tensor("out_0_dram", (rows + P, shape[2]), F32, kind="ExternalOutput").ap()
    build(nc, aps, out)
    r = _run(nc, [arrays], core_ids=[0])
    return r.results[0]["out_0_dram"][:rows].reshape(shape)
```
